# Optimizing a Trainium2 kernel written in Bass

```python
import numpy as np
import jax
import jax.numpy as jnp

def _softmax(x, axis=-1):
    return jax.nn.softmax(x, axis=axis)

def _gelu(x):
    return jax.nn.gelu(x, approximate=True)

def _silu(x):
    return jax.nn.silu(x)

def _sigmoid(x):
    return jax.nn.sigmoid(x)

def _layernorm(x, axis=-1, eps=1e-05):
    m = jnp.mean(x, axis=axis, keepdims=True)
    v = jnp.var(x, axis=axis, keepdims=True)
    return (x - m) / jnp.sqrt(v + eps)

def _scatter_add(tgt, idx, src, axis=0):
    return tgt.at[idx].add(src)

def _segment_sum(src, seg, n):
    return jax.ops.segment_sum(src, seg, n)
kernel_name = 'mk_adaln_d2_jaxref_r8_d679cc'

def setup_inputs(seed: int=0):
    np.random.seed(seed)
    _w = jnp.asarray

    def _L0_attn_setup():
        import jax, jax.numpy as jnp
        import numpy as np
        EMB = 128
        HEADS = 16
        ATT = EMB // HEADS
        key = jax.random.key(seed)
        ks = jax.random.split(key, 5)
        s = 1.0 / np.sqrt(EMB)
        return {'x': jax.random.normal(ks[0], (4, 256, EMB), dtype=jnp.float32), 'Wq': jax.random.uniform(ks[1], (EMB, HEADS * ATT), jnp.float32, -s, s), 'Wk': jax.random.uniform(ks[2], (EMB, HEADS * ATT), jnp.float32, -s, s), 'Wv': jax.random.uniform(ks[3], (EMB, HEADS * ATT), jnp.float32, -s, s), 'Wo': jax.random.uniform(ks[4], (HEADS * ATT, EMB), jnp.float32, -s, s)}
    _L0_attn_in = _L0_attn_setup()

    def _L0_ffn_setup():
        import jax, jax.numpy as jnp
        import numpy as np
        DIM = 128
        INTER = 256
        E = 8
        TOPK = 2
        ROUTE_SCALE = 1.0

        def _mlp(x, w1, w2, w3):
            h = jax.nn.silu(x @ w1.T) * (x @ w3.T)
            return h @ w2.T
        key = jax.random.key(seed)
        ks = jax.random.split(key, 10)
        s_in = 0.02
        return {'x': jax.random.normal(ks[0], (4, 256, DIM), dtype=jnp.float32), 'gate_w': jax.random.normal(ks[1], (E, DIM), dtype=jnp.float32) * s_in, 'gate_bias': jax.random.normal(ks[2], (E,), dtype=jnp.float32) * 0.01, 'w1': jax.random.normal(ks[3], (E, INTER, DIM), dtype=jnp.float32) * s_in, 'w2': jax.random.normal(ks[4], (E, DIM, INTER), dtype=jnp.float32) * s_in, 'w3': jax.random.normal(ks[5], (E, INTER, DIM), dtype=jnp.float32) * s_in, 'sw1': jax.random.normal(ks[6], (INTER, DIM), dtype=jnp.float32) * s_in, 'sw2': jax.random.normal(ks[7], (DIM, INTER), dtype=jnp.float32) * s_in, 'sw3': jax.random.normal(ks[8], (INTER, DIM), dtype=jnp.float32) * s_in}
    _L0_ffn_in = _L0_ffn_setup()
    _L0_c = _w((lambda *s: np.random.randn(*s).astype(np.float32) * 0.05)(4, 128))
    _L0_wmod = _w((lambda *s: np.random.randn(*s).astype(np.float32) * 0.05)(128, 6 * 128) * 128 ** (-0.5))

    def _L1_attn_setup():
        import jax, jax.numpy as jnp
        import numpy as np
        import math
        D = 128
        H = 16
        DH = D // H

        def sinusoidal_pe(length, d):
            pos = jnp.arange(length, dtype=jnp.float32)[:, None]
            div = jnp.exp(jnp.arange(0, d, 2, dtype=jnp.float32) * (-math.log(10000.0) / d))
            ang = pos * div
            return jnp.stack([jnp.sin(ang), jnp.cos(ang)], axis=-1).reshape(length, d)

        def _relative_shift(pos_score):
            B, Hh, S1, S2 = pos_score.shape
            padded = jnp.concatenate([jnp.zeros((B, Hh, S1, 1), pos_score.dtype), pos_score], axis=-1)
            padded = padded.reshape(B, Hh, S2 + 1, S1)
            return padded[:, :, 1:].reshape(B, Hh, S1, S2)
        key = jax.random.key(seed)
        ks = jax.random.split(key, 12)
        s = 0.02
        x = jax.random.normal(ks[0], (2, 256, D), dtype=jnp.float32)
        return {'x': x, 'ln_g': jnp.ones((D,), jnp.float32), 'ln_b': jnp.zeros((D,), jnp.float32), 'Wq': jax.random.normal(ks[1], (D, D), jnp.float32) * s, 'bq': jnp.zeros((D,), jnp.float32), 'Wk': jax.random.normal(ks[2], (D, D), jnp.float32) * s, 'bk': jnp.zeros((D,), jnp.float32), 'Wv': jax.random.normal(ks[3], (D, D), jnp.float32) * s, 'bv': jnp.zeros((D,), jnp.float32), 'Wp': jax.random.normal(ks[4], (D, D), jnp.float32) * s, 'Wo': jax.random.normal(ks[5], (D, D), jnp.float32) * s, 'bo': jnp.zeros((D,), jnp.float32), 'u_bias': jax.random.normal(ks[6], (H, DH), jnp.float32) * 0.05, 'v_bias': jax.random.normal(ks[7], (H, DH), jnp.float32) * 0.05}
    _L1_attn_in = _L1_attn_setup()

    def _L1_ffn_setup():
        import jax, jax.numpy as jnp
        import numpy as np
        H = 128
        E = 64
        K = 8
        G = 8
        TOPK_GROUP = 4
        I_MOE = 64
        I_SHARED = 256
        SCALE = 2.5

        def relu2(x):
            return jnp.square(jax.nn.relu(x))

        def _route(xf, router_w, correction_bias):
            T = xf.shape[0]
            logits = xf @ router_w.T
            scores = jax.nn.sigmoid(logits)
            sfc = scores + correction_bias[None, :]
            grp = sfc.reshape(T, G, E // G)
            top2, _ = jax.lax.top_k(grp, 2)
            group_scores = top2.sum(-1)
            _, gidx = jax.lax.top_k(group_scores, TOPK_GROUP)
            gmask = jnp.zeros((T, G), sfc.dtype).at[jnp.arange(T)[:, None], gidx].set(1.0)
            emask = jnp.repeat(gmask, E // G, axis=1)
            masked = jnp.where(emask > 0, sfc, 0.0)
            _, tidx = jax.lax.top_k(masked, K)
            tw = jnp.take_along_axis(scores, tidx, axis=1)
            tw = tw / (tw.sum(-1, keepdims=True) + 1e-20)
            return (tidx, tw * SCALE)
        key = jax.random.key(seed)
        ks = jax.random.split(key, 7)
        x = jax.random.normal(ks[0], (2, 128, H), dtype=jnp.float32)
        router_w = jax.random.normal(ks[1], (E, H), dtype=jnp.float32) * 0.02
        correction_bias = jax.random.normal(ks[2], (E,), dtype=jnp.float32) * 0.01
        up_w = jax.random.normal(ks[3], (E, H, I_MOE), dtype=jnp.float32) * 0.02
        down_w = jax.random.normal(ks[4], (E, I_MOE, H), dtype=jnp.float32) * 0.02
        shared_up_w = jax.random.normal(ks[5], (H, I_SHARED), dtype=jnp.float32) * 0.02
        shared_down_w = jax.random.normal(ks[6], (I_SHARED, H), dtype=jnp.float32) * 0.02
        return {'x': x, 'router_w': router_w, 'correction_bias': correction_bias, 'up_w': up_w, 'down_w': down_w, 'shared_up_w': shared_up_w, 'shared_down_w': shared_down_w}
    _L1_ffn_in = _L1_ffn_setup()
    _L1_c = _w((lambda *s: np.random.randn(*s).astype(np.float32) * 0.05)(4, 128))
    _L1_wmod = _w((lambda *s: np.random.randn(*s).astype(np.float32) * 0.05)(128, 6 * 128) * 128 ** (-0.5))
    _d = {'L0_attn_x': _L0_attn_in['x'], 'L0_attn_Wq': _L0_attn_in['Wq'], 'L0_attn_Wk': _L0_attn_in['Wk'], 'L0_attn_Wv': _L0_attn_in['Wv'], 'L0_attn_Wo': _L0_attn_in['Wo'], 'L0_ffn_gate_w': _L0_ffn_in['gate_w'], 'L0_ffn_gate_bias': _L0_ffn_in['gate_bias'], 'L0_ffn_w1': _L0_ffn_in['w1'], 'L0_ffn_w2': _L0_ffn_in['w2'], 'L0_ffn_w3': _L0_ffn_in['w3'], 'L0_ffn_sw1': _L0_ffn_in['sw1'], 'L0_ffn_sw2': _L0_ffn_in['sw2'], 'L0_ffn_sw3': _L0_ffn_in['sw3'], 'L0_c': _L0_c, 'L0_wmod': _L0_wmod, 'L1_attn_ln_g': _L1_attn_in['ln_g'], 'L1_attn_ln_b': _L1_attn_in['ln_b'], 'L1_attn_Wq': _L1_attn_in['Wq'], 'L1_attn_bq': _L1_attn_in['bq'], 'L1_attn_Wk': _L1_attn_in['Wk'], 'L1_attn_bk': _L1_attn_in['bk'], 'L1_attn_Wv': _L1_attn_in['Wv'], 'L1_attn_bv': _L1_attn_in['bv'], 'L1_attn_Wp': _L1_attn_in['Wp'], 'L1_attn_Wo': _L1_attn_in['Wo'], 'L1_attn_bo': _L1_attn_in['bo'], 'L1_attn_u_bias': _L1_attn_in['u_bias'], 'L1_attn_v_bias': _L1_attn_in['v_bias'], 'L1_ffn_router_w': _L1_ffn_in['router_w'], 'L1_ffn_correction_bias': _L1_ffn_in['correction_bias'], 'L1_ffn_up_w': _L1_ffn_in['up_w'], 'L1_ffn_down_w': _L1_ffn_in['down_w'], 'L1_ffn_shared_up_w': _L1_ffn_in['shared_up_w'], 'L1_ffn_shared_down_w': _L1_ffn_in['shared_down_w'], 'L1_c': _L1_c, 'L1_wmod': _L1_wmod}
    _x0 = _d['L0_attn_x']
    _d['L0_attn_x'] = jax.random.normal(jax.random.fold_in(jax.random.key(seed), 1), (4, 512, 128), dtype=_x0.dtype)
    del _x0
    return _d

def reference(L0_attn_x, L0_attn_Wq, L0_attn_Wk, L0_attn_Wv, L0_attn_Wo, L0_ffn_gate_w, L0_ffn_gate_bias, L0_ffn_w1, L0_ffn_w2, L0_ffn_w3, L0_ffn_sw1, L0_ffn_sw2, L0_ffn_sw3, L0_c, L0_wmod, L1_attn_ln_g, L1_attn_ln_b, L1_attn_Wq, L1_attn_bq, L1_attn_Wk, L1_attn_bk, L1_attn_Wv, L1_attn_bv, L1_attn_Wp, L1_attn_Wo, L1_attn_bo, L1_attn_u_bias, L1_attn_v_bias, L1_ffn_router_w, L1_ffn_correction_bias, L1_ffn_up_w, L1_ffn_down_w, L1_ffn_shared_up_w, L1_ffn_shared_down_w, L1_c, L1_wmod):

    def _L0_attn_ref(x, Wq, Wk, Wv, Wo):
        import jax, jax.numpy as jnp
        import numpy as np
        EMB = 128
        HEADS = 16
        ATT = EMB // HEADS
        b, t, _ = x.shape
        h, d = (HEADS, ATT)
        scale = d ** (-0.25)
        q = (x @ Wq).reshape(b, t, h, d) * scale
        k = (x @ Wk).reshape(b, t, h, d) * scale
        v = (x @ Wv).reshape(b, t, h, d)
        dot = jnp.einsum('bqhd,bkhd->bhqk', q, k)
        causal = jnp.tril(jnp.ones((t, t), dtype=bool))
        dot = jnp.where(causal[None, None], dot, -jnp.inf)
        attn = jax.nn.softmax(dot, axis=-1)
        out = jnp.einsum('bhqk,bkhd->bqhd', attn, v).reshape(b, t, h * d)
        return out @ Wo

    def _L0_ffn_ref(x, gate_w, gate_bias, w1, w2, w3, sw1, sw2, sw3):
        import jax, jax.numpy as jnp
        import numpy as np
        DIM = 128
        INTER = 256
        E = 8
        TOPK = 2
        ROUTE_SCALE = 1.0

        def _mlp(x, w1, w2, w3):
            h = jax.nn.silu(x @ w1.T) * (x @ w3.T)
            return h @ w2.T
        shape = x.shape
        xt = x.reshape(-1, DIM)
        T = xt.shape[0]
        logits = xt @ gate_w.T
        scores = jax.nn.softmax(logits.astype(jnp.float32), axis=-1)
        original_scores = scores
        biased = scores + gate_bias
        _, indices = jax.lax.top_k(biased, TOPK)
        weights = jnp.take_along_axis(original_scores, indices, axis=1)
        weights = (weights * ROUTE_SCALE).astype(x.dtype)
        combine = (jax.nn.one_hot(indices, E, dtype=weights.dtype) * weights[..., None]).sum(axis=1)
        y = jnp.zeros_like(xt)
        for e in range(E):
            y = y + _mlp(xt, w1[e], w2[e], w3[e]) * combine[:, e:e + 1]
        z = _mlp(xt, sw1, sw2, sw3)
        return (y + z).reshape(shape)

    def _L1_attn_ref(x, ln_g, ln_b, Wq, bq, Wk, bk, Wv, bv, Wp, Wo, bo, u_bias, v_bias):
        import jax, jax.numpy as jnp
        import numpy as np
        import math
        D = 128
        H = 16
        DH = D // H

        def sinusoidal_pe(length, d):
            pos = jnp.arange(length, dtype=jnp.float32)[:, None]
            div = jnp.exp(jnp.arange(0, d, 2, dtype=jnp.float32) * (-math.log(10000.0) / d))
            ang = pos * div
            return jnp.stack([jnp.sin(ang), jnp.cos(ang)], axis=-1).reshape(length, d)

        def _relative_shift(pos_score):
            B, Hh, S1, S2 = pos_score.shape
            padded = jnp.concatenate([jnp.zeros((B, Hh, S1, 1), pos_score.dtype), pos_score], axis=-1)
            padded = padded.reshape(B, Hh, S2 + 1, S1)
            return padded[:, :, 1:].reshape(B, Hh, S1, S2)
        B, S, Dm = x.shape
        dh = Dm // H
        scale = dh ** (-0.5)
        pe = sinusoidal_pe(S, Dm)
        mu = jnp.mean(x, axis=-1, keepdims=True)
        var = jnp.var(x, axis=-1, keepdims=True)
        xn = (x - mu) / jnp.sqrt(var + 1e-05) * ln_g + ln_b
        q = (xn @ Wq + bq).reshape(B, S, H, dh)
        k = (xn @ Wk + bk).reshape(B, S, H, dh)
        v = (xn @ Wv + bv).reshape(B, S, H, dh)
        p = (pe @ Wp).reshape(S, H, dh)
        content = jnp.einsum('bihd,bjhd->bhij', q + u_bias, k)
        pos = jnp.einsum('bihd,jhd->bhij', q + v_bias, p)
        pos = _relative_shift(pos)
        attn = jax.nn.softmax((content + pos) * scale, axis=-1)
        head = jnp.einsum('bhij,bjhd->bihd', attn, v).reshape(B, S, Dm)
        return head @ Wo + bo

    def _L1_ffn_ref(x, router_w, correction_bias, up_w, down_w, shared_up_w, shared_down_w):
        import jax, jax.numpy as jnp
        import numpy as np
        H = 128
        E = 64
        K = 8
        G = 8
        TOPK_GROUP = 4
        I_MOE = 64
        I_SHARED = 256
        SCALE = 2.5

        def relu2(x):
            return jnp.square(jax.nn.relu(x))

        def _route(xf, router_w, correction_bias):
            T = xf.shape[0]
            logits = xf @ router_w.T
            scores = jax.nn.sigmoid(logits)
            sfc = scores + correction_bias[None, :]
            grp = sfc.reshape(T, G, E // G)
            top2, _ = jax.lax.top_k(grp, 2)
            group_scores = top2.sum(-1)
            _, gidx = jax.lax.top_k(group_scores, TOPK_GROUP)
            gmask = jnp.zeros((T, G), sfc.dtype).at[jnp.arange(T)[:, None], gidx].set(1.0)
            emask = jnp.repeat(gmask, E // G, axis=1)
            masked = jnp.where(emask > 0, sfc, 0.0)
            _, tidx = jax.lax.top_k(masked, K)
            tw = jnp.take_along_axis(scores, tidx, axis=1)
            tw = tw / (tw.sum(-1, keepdims=True) + 1e-20)
            return (tidx, tw * SCALE)
        B, S, Hd = x.shape
        xf = x.reshape(-1, Hd)
        T = xf.shape[0]
        tidx, tw = _route(xf.astype(jnp.float32), router_w, correction_bias)
        combine = jnp.zeros((T, E), xf.dtype).at[jnp.arange(T)[:, None], tidx].add(tw.astype(xf.dtype))

        def body(acc, ew):
            wu, wd, c = ew
            return (acc + c[:, None] * (relu2(xf @ wu) @ wd), None)
        routed, _ = jax.lax.scan(body, jnp.zeros_like(xf), (up_w, down_w, combine.T))
        shared = relu2(xf @ shared_up_w) @ shared_down_w
        return (routed + shared).reshape(B, S, Hd)
    x = L0_attn_x
    mod = (_silu(L0_c) @ L0_wmod).reshape(L0_c.shape[0], 6, 1, -1)
    sa, ca, ga, sb, cb, gb = (mod[:, 0], mod[:, 1], mod[:, 2], mod[:, 3], mod[:, 4], mod[:, 5])
    ga = (2 * (ga >= 0) - 1) * jnp.maximum(jnp.abs(ga), 0.25)
    gb = (2 * (gb >= 0) - 1) * jnp.maximum(jnp.abs(gb), 0.25)
    h = _layernorm(x, axis=-1) * (1 + ca) + sa
    x = x + ga * _L0_attn_ref(h, L0_attn_Wq, L0_attn_Wk, L0_attn_Wv, L0_attn_Wo)
    h = _layernorm(x, axis=-1) * (1 + cb) + sb
    x = x + gb * _L0_ffn_ref(h, L0_ffn_gate_w, L0_ffn_gate_bias, L0_ffn_w1, L0_ffn_w2, L0_ffn_w3, L0_ffn_sw1, L0_ffn_sw2, L0_ffn_sw3)
    mod = (_silu(L1_c) @ L1_wmod).reshape(L1_c.shape[0], 6, 1, -1)
    sa, ca, ga, sb, cb, gb = (mod[:, 0], mod[:, 1], mod[:, 2], mod[:, 3], mod[:, 4], mod[:, 5])
    ga = (2 * (ga >= 0) - 1) * jnp.maximum(jnp.abs(ga), 0.25)
    gb = (2 * (gb >= 0) - 1) * jnp.maximum(jnp.abs(gb), 0.25)
    h = _layernorm(x, axis=-1) * (1 + ca) + sa
    x = x + ga * _L1_attn_ref(h, L1_attn_ln_g, L1_attn_ln_b, L1_attn_Wq, L1_attn_bq, L1_attn_Wk, L1_attn_bk, L1_attn_Wv, L1_attn_bv, L1_attn_Wp, L1_attn_Wo, L1_attn_bo, L1_attn_u_bias, L1_attn_v_bias)
    h = _layernorm(x, axis=-1) * (1 + cb) + sb
    x = x + gb * _L1_ffn_ref(h, L1_ffn_router_w, L1_ffn_correction_bias, L1_ffn_up_w, L1_ffn_down_w, L1_ffn_shared_up_w, L1_ffn_shared_down_w)
    return x

_drawn_inputs = setup_inputs


def setup_inputs(seed=0):
    import zlib

    import numpy as np

    out = dict(_drawn_inputs(seed))
    spreads = {'L1_attn_ln_g': (1.0, 0.6),
     'L1_attn_ln_b': (0.0, 0.8),
     'L1_attn_bq': (0.0, 0.8),
     'L1_attn_bk': (0.0, 0.8),
     'L1_attn_bv': (0.0, 0.8),
     'L1_attn_bo': (0.0, 0.341)}
    factors = {'L0_attn_Wq': 8.0,
     'L0_attn_Wk': 8.0,
     'L0_attn_Wv': 5.56,
     'L0_attn_Wo': 5.576,
     'L0_ffn_gate_w': 8.0,
     'L0_ffn_gate_bias': 8.0,
     'L0_ffn_w1': 8.0,
     'L0_ffn_w2': 8.0,
     'L0_ffn_w3': 8.0,
     'L0_ffn_sw1': 8.0,
     'L0_ffn_sw2': 8.0,
     'L0_ffn_sw3': 8.0,
     'L0_c': 5.5,
     'L0_wmod': 5.741,
     'L1_attn_Wq': 8.0,
     'L1_attn_Wk': 8.0,
     'L1_attn_Wv': 8.0,
     'L1_attn_Wp': 8.0,
     'L1_attn_Wo': 8.0,
     'L1_attn_u_bias': 8.0,
     'L1_attn_v_bias': 8.0,
     'L1_ffn_router_w': 8.0,
     'L1_ffn_correction_bias': 8.0,
     'L1_ffn_up_w': 8.0,
     'L1_ffn_down_w': 8.0,
     'L1_ffn_shared_up_w': 8.0,
     'L1_ffn_shared_down_w': 8.0}
    for name, (base, spread) in spreads.items():
        noise = np.random.default_rng([zlib.crc32(name.encode()), seed]).standard_normal(out[name].shape)
        drawn = base * np.exp(spread * noise) if base else spread * noise
        out[name] = jnp.asarray(drawn.astype(out[name].dtype))
    for name, factor in factors.items():
        out[name] = (out[name] * factor).astype(out[name].dtype)
    return out
```

```python
from contextlib import ExitStack

import numpy as np

import concourse.bass as bass
from concourse import mybir

P = 128
F32 = mybir.dt.float32
F32R = mybir.dt.float32r
BF16 = mybir.dt.bfloat16
U32 = mybir.dt.uint32
ALU = mybir.AluOpType
ACT = mybir.ActivationFunctionType
AX_X = mybir.AxisListType.X

B, T, D = 4, 512, 128
NTOK = B * T
H, DH = 16, 8
HG = 4
NG = H // HG
NIT = B * NG
NB = T // P
DIAG = P + 1
QW = 32
LN_EPS = 1e-5
NEG = -1e30


class Cfg:

    def __init__(self, rel):
        self.rel = rel
        self.scale = float(DH) ** -0.5
        self.E = 64 if rel else 8
        self.up = 1 if rel else 2
        self.units = 32 if rel else 16


def wait_past(eng, sem, value):
    if isinstance(value, int) and value <= 0:
        return
    eng.wait_ge(sem, value)


def add_layernorm(nc, name, src, dst, mul, add, ones, eps, dst_hi=None, dst_lo=None, wv=None, bv=None, vall=None, counts=None):
    with ExitStack() as ctx:
        sb = lambda n, s, d=F32: ctx.enter_context(nc.sbuf_tensor(f"{name}_{n}", s, d))
        mean_ps = ctx.enter_context(nc.psum_tensor(f"{name}_mean", [P, B, T], F32))
        var_ps = ctx.enter_context(nc.psum_tensor(f"{name}_var", [P, B, T], F32))
        xc = sb("xc", [P, B, T])
        sq = sb("sq", [P, B, T])
        std, rstd = sb("std", [P, B, T]), sb("rstd", [P, B, T])
        norm = sb("norm", [P, B, T])
        names = ("mean_ready", "centered", "squared", "var_ready", "std_ready", "rstd_ready", "norm_ready", "out_ready")
        names += (("hi_ready", "lo_ready") if dst_hi is not None else ()) + (("v_ready",) if wv is not None else ())
        sem, base = {}, {}
        for n in names:
            sem[n], base[n] = counts.setdefault(n, (None, 0))
            if sem[n] is None:
                sem[n] = nc.alloc_semaphore(f"ln_{n}")
            counts[n] = (sem[n], base[n] + B)

        def wait(eng, n, value):
            eng.wait_ge(sem[n], base[n] + value)

        block = ctx.enter_context(nc.Block())

        def v_of(b, t):
            return mean_ps[:, b, t * P:(t + 1) * P].rearrange("p (h d) -> p h d", d=DH)

        @block.tensor
        def _(pe):
            for b in range(B):
                pe.matmul(mean_ps[:, b, :], ones[:], src[:, b * T:(b + 1) * T], start=True, stop=True).then_inc(sem["mean_ready"], 1)
            for b in range(B):
                wait(pe, "squared", b + 1)
                pe.matmul(var_ps[:, b, :], ones[:], sq[:, b, :], start=True, stop=True).then_inc(sem["var_ready"], 1)
            if wv is not None:
                for b in range(B):
                    wait(pe, "out_ready", b + 1)
                    wait(pe, "centered", b + 1)
                    for t in range(NB):
                        lo = b * T + t * P
                        mm = pe.matmul(mean_ps[:, b, t * P:(t + 1) * P], dst[:, lo:lo + P], wv[:], start=True, stop=True)
                    mm.then_inc(sem["v_ready"], 1)

        @block.scalar
        def _(act):
            for b in range(B):
                wait(act, "centered", b + 1)
                act.activation(sq[:, b, :], xc[:, b, :], ACT.Square).then_inc(sem["squared"], 1)
            for b in range(B):
                wait(act, "var_ready", b + 1)
                act.activation(std[:, b, :], var_ps[:, b, :], ACT.Sqrt, bias=eps[:, 0:1]).then_inc(sem["std_ready"], 1)
            if wv is not None and bv is None:
                for b in range(B):
                    wait(act, "v_ready", b + 1)
                    for t in range(NB):
                        act.copy(vall[:, b * NB + t, :, 0:DH], v_of(b, t))

        @block.vector
        def _(ve):
            for b in range(B):
                wait(ve, "mean_ready", b + 1)
                ve.tensor_tensor(xc[:, b, :], src[:, b * T:(b + 1) * T], mean_ps[:, b, :], ALU.subtract).then_inc(sem["centered"], 1)
            for b in range(B):
                wait(ve, "std_ready", b + 1)
                ve.reciprocal(rstd[:, b, :], std[:, b, :]).then_inc(sem["rstd_ready"], 1)
                wait(ve, "rstd_ready", b + 1)
                ve.tensor_tensor(norm[:, b, :], xc[:, b, :], rstd[:, b, :], ALU.mult).then_inc(sem["norm_ready"], 1)
                wait(ve, "norm_ready", b + 1)
                ve.tensor_scalar(dst[:, b * T:(b + 1) * T], norm[:, b, :], mul(b), add(b), ALU.mult, ALU.add).then_inc(sem["out_ready"], 1)
                if dst_hi is not None:
                    wait(ve, "out_ready", b + 1)
                    ve.tensor_copy(dst_hi[:, b * T:(b + 1) * T], dst[:, b * T:(b + 1) * T]).then_inc(sem["hi_ready"], 1)
            if bv is not None:
                for b in range(B):
                    wait(ve, "v_ready", b + 1)
                    for t in range(NB):
                        ve.tensor_tensor(vall[:, b * NB + t, :, 0:DH], v_of(b, t), bv[:].rearrange("p (h d) -> p h d", d=DH), ALU.add)

        @block.gpsimd
        def _(pool):
            if dst_lo is not None:
                for b in range(B):
                    wait(pool, "hi_ready", b + 1)
                    s = slice(b * T, (b + 1) * T)
                    pool.tensor_tensor(dst_lo[:, s], dst[:, s], dst_hi[:, s].bitcast(F32), ALU.subtract).then_inc(sem["lo_ready"], 1)


def add_modulation(nc, layers):
    with ExitStack() as ctx:
        sem = lambda n: nc.alloc_semaphore(f"mod_{n}")
        loaded, silu_ready, made, copied, step = sem("ld"), sem("silu"), sem("mm"), sem("cp"), sem("step")
        tiles = []
        for k, (cT, wmod, mod) in enumerate(layers):
            tiles.append((
                ctx.enter_context(nc.sbuf_tensor(f"mod_c{k}", [P, B], F32)),
                ctx.enter_context(nc.sbuf_tensor(f"mod_s{k}", [P, B], F32)),
                ctx.enter_context(nc.sbuf_tensor(f"mod_w{k}", [P, 6 * D], F32)),
                ctx.enter_context(nc.sbuf_tensor(f"mod_sg{k}", [P, 2, B], F32)),
                ctx.enter_context(nc.sbuf_tensor(f"mod_mg{k}", [P, 2, B], F32)),
                ctx.enter_context(nc.psum_tensor(f"mod_p{k}", [P, 6, B], F32)),
            ))
        n = len(layers)
        block = ctx.enter_context(nc.Block())

        @block.sync
        def _(sp):
            for (cT, wmod, _), t in zip(layers, tiles):
                sp.dma_start(t[0][:], cT).then_inc(loaded, 16)
                sp.dma_start(t[2][:], wmod).then_inc(loaded, 16)

        @block.scalar
        def _(act):
            act.wait_ge(loaded, 32 * n)
            for t in tiles:
                act.activation(t[1][:], t[0][:], ACT.Silu).then_inc(silu_ready, 1)

        @block.tensor
        def _(pe):
            pe.wait_ge(silu_ready, n)
            for t in tiles:
                for k in range(6):
                    mm = pe.matmul(t[5][:, k, :], t[2][:, k * D:(k + 1) * D], t[1][:], start=True, stop=True)
                mm.then_inc(made, 1)

        @block.vector
        def _(ve):
            for k, ((_, _, mod), t) in enumerate(zip(layers, tiles)):
                ve.wait_ge(made, k + 1)
                ve.tensor_copy(mod[:], t[5][:]).then_inc(copied, 1)
                ve.wait_ge(copied, k + 1)
                sg, mg = t[3], t[4]
                gates = mod[:, 2::3, :]
                gains = mod[:, 1::3, :]
                ve.tensor_scalar(sg[:], gates, 0.0, 2.0, ALU.is_ge, ALU.mult).then_inc(step, 1)
                ve.tensor_scalar(mg[:], gates, -1.0, None, ALU.mult).then_inc(step, 1)
                ve.tensor_scalar(gains, gains, 1.0, None, ALU.add).then_inc(step, 1)
                ve.wait_ge(step, 5 * k + 3)
                ve.scalar_tensor_tensor(out=mg[:], in0=mg[:], scalar=0.25, in1=gates, op0=ALU.max, op1=ALU.max).then_inc(step, 1)
                ve.wait_ge(step, 5 * k + 4)
                ve.scalar_tensor_tensor(out=gates, in0=sg[:], scalar=-1.0, in1=mg[:], op0=ALU.add, op1=ALU.mult).then_inc(step, 1)


def add_attention(nc, cfg, xT, hT, vall, gate, consts, dram):
    rel = cfg.rel
    name = "rel" if rel else "cau"
    with ExitStack() as ctx:
        sb = lambda n, s, d=F32: ctx.enter_context(nc.sbuf_tensor(f"{name}_{n}", s, d))
        sem = lambda n: nc.alloc_semaphore(f"{name}_{n}")
        ps = ctx.enter_context(nc.psum_tensor(f"{name}_ps", [P, 8, T], F32))
        S = lambda i: ps[:, i, :]
        BANK_A, BANK_B, BANK_T = ps[:, 4, :], ps[:, 5, :], lambda j: ps[:, 6 + j % 2, :]

        wqk = sb("wqk", [P, 2, P])
        wo = sb("wo", [P, P])
        vcur = sb("vcur", [P, NB, HG, QW])
        qs, ks = sb("qs", [P, T]), sb("ks", [P, T])
        q_hi, k_hi = sb("qhi", [P, T], F32R), sb("khi", [P, T], F32R)
        qz = sb("qz", [P, HG, T], F32R)
        kst = sb("kst", [P, T], F32R)
        probs = sb("probs", [P, 2, NB, T])
        negmax = sb("negmax", [P, HG, NB])
        pT = sb("pT", [P, HG, NB, T])
        o_sb, recip, o_norm = sb("o", [P, T]), sb("recip", [P, T]), sb("onorm", [P, T])
        if rel:
            as_, a_hi, ast = sb("as", [P, T]), sb("ahi", [P, T], F32R), sb("ast", [P, T], F32R)
            wp_raw = sb("wpraw", [P, HG * 2 * P])
            wp_hi = sb("wphi", [P, HG * 2 * P], F32R)
            wp_all = sb("wpall", [P, NG, HG * 2 * P], F32R)
            wp = sb("wp", [P, HG, 2, P], F32R)
            rot1, rot2 = sb("rot1", [P, T]), sb("rot2", [P, T])
            gT = sb("gT", [P, T + 1])
            diag = sb("diag", [P, 2, DIAG])
            dsum = sb("dsum", [P, DIAG])
            cols = sb("cols", [P, 5, NG])
            bqu, bqv, bks = sb("bqu", [P, NG]), sb("bqv", [P, NG]), sb("bks", [P, NG])
            gbo = sb("gbo", [P, B])

        wqk_loaded, wo_loaded, v_loaded = sem("wqk"), sem("wo"), sem("v")
        proj_ready, q_scaled, hi_copied, stacked = sem("proj"), sem("qsc"), sem("hi"), sem("stk")
        scores_ready, max_ready, exp_ready = sem("sc"), sem("mx"), sem("exp")
        turned, turned_copied = sem("tr"), sem("trc")
        pv_ready, o_copied, sums_ready, recip_ready, o_normed = sem("pv"), sem("oc"), sem("sum"), sem("rec"), sem("on")
        wo_done, x_added = sem("wod"), sem("xa")
        if rel:
            wp_loaded, once, bias_step = sem("wp"), sem("once"), sem("bst")
            g_ready, rotated, g_summed = sem("g"), sem("rot"), sem("gs")
            diag_masked, diag_summed, diag_added = sem("dm"), sem("ds"), sem("da")
            wp_split, wp_kept = sem("wps"), sem("wpk")
        NSTK = HG + 1 + rel
        NPROJ = 2 + rel

        with nc.Block() as setup:
            @setup.sync
            def _(sp):
                if rel:
                    sp.dma_start(cols[:], dram["cols"]).then_inc(once, 16)
                    for g in range(NG):
                        wait_past(sp, wp_split, g)
                        sp.dma_start(wp_raw[:], dram["wp"][g]).then_inc(wp_kept, 16)

            @setup.gpsimd
            def _(pool):
                pool.memset(qz[:].bitcast(F32), 0.0)
                if rel:
                    pool.memset(gT[:, T:T + 1], 0.0)

            @setup.vector
            def _(ve):
                if not rel:
                    return
                ve.wait_ge(once, 16)
                ve.tensor_tensor(rot1[:, 0:NG], cols[:, 0, :], cols[:, 1, :], ALU.add).then_inc(bias_step, 1)
                ve.tensor_tensor(rot2[:, 0:NG], cols[:, 0, :], cols[:, 2, :], ALU.add).then_inc(bias_step, 1)
                ve.tensor_scalar(gbo[:], gate, cols[:, 4, 0:1], None, ALU.mult).then_inc(bias_step, 1)
                ve.tensor_copy(bks[:], cols[:, 3, :])
                ve.wait_ge(bias_step, 3)
                ve.tensor_scalar(bqu[:], rot1[:, 0:NG], cfg.scale, None, ALU.mult)
                ve.tensor_scalar(bqv[:], rot2[:, 0:NG], cfg.scale, None, ALU.mult)
                for b in range(B):
                    s = slice(b * T, (b + 1) * T)
                    ve.tensor_scalar(xT[:, s], xT[:, s], gbo[:, b:b + 1], None, ALU.add)
                for g in range(NG):
                    ve.wait_ge(wp_kept, 16 * (g + 1))
                    wait_past(ve, wp_split, g)
                    ve.tensor_copy(wp_hi[:], wp_raw[:]).then_inc(hi_copied, 1)
                    ve.wait_ge(hi_copied, g + 1)
                    ve.scalar_tensor_tensor(out=wp_all[:, g, :], in0=wp_hi[:].bitcast(F32), scalar=consts["neg_lo_k"],
                                            in1=wp_raw[:], op0=ALU.mult, op1=ALU.add).then_inc(wp_split, 1)

        block = ctx.enter_context(nc.Block())

        def peeled(body):
            body(0, False)

            def rest(eng):
                with eng.Fori(1, NIT - 1) as n:
                    body(n, False)
                body(NIT - 1, True)
            return rest

        @block.sync
        def _(sp):
            def body(n, last):
                wait_past(sp, proj_ready, 2 * n)
                sp.dma_start(wqk[:], dram["wqk"][bass.ds(n % NG, 1)].rearrange("o p (k m) -> p (o k) m", k=2)).then_inc(wqk_loaded, 16)
                if rel:
                    wait_past(sp, g_ready, HG * n)
                    sp.dma_start(wp[:].bitcast(F32), wp_all[:, bass.ds(n % NG, 1), :].bitcast(F32).rearrange("p o (h k m) -> p (o h) k m", h=HG, k=2)).then_inc(wp_loaded, 16)
                wait_past(sp, pv_ready, n)
                sp.dma_start(vcur[:], vall[:, bass.ds((n // NG) * NB, NB), bass.ds((n % NG) * HG, HG), :]).then_inc(v_loaded, 16)
                wait_past(sp, wo_done, n)
                sp.dma_start(wo[:], dram["wo"][bass.ds(n % NG, 1)].rearrange("o p m -> p (o m)")).then_inc(wo_loaded, 16)

            peeled(body)(sp)

        @block.tensor
        def _(pe):
            def project(n, n16):
                pe.wait_ge(wqk_loaded, n16)
                if rel:
                    wait_past(pe, diag_masked, HG * NB * n)
                moving = hT[:, bass.ds((n // NG) * T, T)]
                pe.matmul(BANK_A, wqk[:, 0, :], moving, start=True, stop=True).then_inc(proj_ready, 1)
                pe.matmul(BANK_B, wqk[:, 1, :], moving, start=True, stop=True).then_inc(proj_ready, 1)

            def transposes(n, h, j):
                base = HG * NB * n + NB * h
                pe.wait_ge(exp_ready, base + NB)
                wait_past(pe, turned_copied, base + j - 1)
                for i in range(0 if rel else j, NB):
                    tr = pe.transpose(BANK_T(j)[:, i * P:(i + 1) * P], probs[:, h % 2, i, j * P:(j + 1) * P], consts["ident"])
                tr.then_inc(turned, 1)

            def head_scores(n, h):
                base = HG * NB * n + NB * h
                if h == 0:
                    pe.wait_ge(stacked, NSTK * (n + 1))
                if rel:
                    if h == 0:
                        pe.wait_ge(wp_loaded, 16 * (n + 1))
                        wait_past(pe, x_added, n)
                    wait_past(pe, diag_masked, base)
                    pe.matmul(BANK_A, wp[:, h, 0, :], ast[:], start=True, stop=True)
                    pe.matmul(BANK_B, wp[:, h, 1, :], ast[:], start=True, stop=True).then_inc(g_ready, 1)
                for i in range(NB):
                    scores(n, h, base, i)
                    if h > 0 and i > 0:
                        transposes(n, h - 1, i - 1)
                if h > 0:
                    transposes(n, h - 1, NB - 1)

            def scores(n, h, base, i):
                    wait_past(pe, exp_ready, base + i + 1 - NB)
                    q = qz[:, h, i * P:(i + 1) * P]
                    if not rel:
                        w = max((i + 1) * P, 2 * P)
                        pe.matmul(S(i)[:, 0:w], q, kst[:, 0:w], start=True, stop=False, skip_group_check=True)
                        mm = pe.matmul(S(i)[:, i * P:(i + 1) * P], consts["ident_bf"], consts["causal"],
                                       start=False, stop=True, skip_group_check=True)
                        mm.then_inc(scores_ready, 1)
                        return
                    d, e = i * P, (i + 1) * P
                    w = min(DIAG, T - d)
                    pe.matmul(S(i), q, kst[:], start=True, stop=False, skip_group_check=True)
                    if i == 0:
                        pe.wait_ge(g_summed, HG * n + h + 1)
                    own, nxt = gT[:, d:d + P], gT[:, d + 1:d + P + 1]
                    if i > 0:
                        pe.matmul(S(i)[:, 0:d], own, consts["pe"][:, T:T + d], start=False, stop=False, skip_group_check=True)
                    if i < NB - 1:
                        pe.matmul(S(i)[:, e + 1:T], nxt, consts["pe"][:, e + 1:T], start=False, stop=False, skip_group_check=True)
                    if i >= 2:
                        pe.wait_ge(diag_masked, base + i - 1)
                    bank = ps[:, 4 + i % 2, :]
                    pe.matmul(bank[:, 0:w], own, consts["pe"][:, T + d:T + d + w], start=True, stop=True, skip_group_check=True)
                    pe.matmul(bank[:, DIAG:DIAG + w], nxt, consts["pe"][:, d:d + w], start=True, stop=True, skip_group_check=True).then_inc(scores_ready, 1)

            def tail(n):
                for j in range(NB):
                    transposes(n, HG - 1, j)
                pe.wait_ge(turned_copied, HG * NB * (n + 1))
                pe.wait_ge(v_loaded, 16 * (n + 1))
                for j in range(NB):
                    i0 = 0 if rel else j * P
                    for h in range(HG):
                        mm = pe.matmul(BANK_A[h * QW:(h + 1) * QW, i0:T], vcur[:, j, h, :], pT[:, h, j, i0:T],
                                       start=(j == 0), stop=(j == NB - 1), skip_group_check=True)
                mm.then_inc(pv_ready, 1)
                pe.wait_ge(o_copied, n + 1)
                pe.matmul(BANK_B, consts["pick"], o_sb[:], start=True, stop=True).then_inc(sums_ready, 1)
                pe.wait_ge(o_normed, n + 1)
                pe.wait_ge(wo_loaded, 16 * (n + 1))
                pe.matmul(BANK_A, wo[:], o_norm[:], start=True, stop=True).then_inc(wo_done, 1)

            def body(n, last):
                for h in range(HG):
                    head_scores(n, h)
                if not last:
                    wait_past(pe, x_added, n)
                    project(n + 1, 16 * (n + 2))
                    pe.wait_ge(q_scaled, NPROJ * (n + 2))
                tail(n)

            project(0, 16)
            peeled(body)(pe)

        @block.scalar
        def _(act):
            def evacuate(n):
                g = n % NG
                pe_n = 2 * n
                act.wait_ge(proj_ready, pe_n + 1)
                wait_past(act, stacked, NSTK * n)
                if rel:
                    act.activation(qs[:], BANK_A, ACT.Identity, bias=bqu[:, bass.ds(g, 1)], scale=cfg.scale).then_inc(q_scaled, 1)
                    act.activation(as_[:], BANK_A, ACT.Identity, bias=bqv[:, bass.ds(g, 1)], scale=cfg.scale).then_inc(q_scaled, 1)
                    act.wait_ge(proj_ready, pe_n + 2)
                    act.activation(ks[:], BANK_B, ACT.Identity, bias=bks[:, bass.ds(g, 1)], scale=1.0).then_inc(q_scaled, 1)
                else:
                    act.mul(qs[:], BANK_A, cfg.scale).then_inc(q_scaled, 1)
                    act.wait_ge(proj_ready, pe_n + 2)
                    act.copy(ks[:], BANK_B).then_inc(q_scaled, 1)

            def exp(n, h, i):
                base = HG * NB * n + NB * h
                if i == 0:
                    wait_past(act, turned, base - NB)
                w = T if rel else (i + 1) * P
                act.wait_ge(max_ready, base + i + 1)
                act.activation(probs[:, h % 2, i, 0:w], S(i)[:, 0:w], ACT.Exp, bias=negmax[:, h, i:i + 1]).then_inc(exp_ready, 1)

            def copy(n, h, j):
                if h == 0 and j == 0:
                    wait_past(act, pv_ready, n)
                i0 = 0 if rel else j * P
                act.wait_ge(turned, HG * NB * n + NB * h + j + 1)
                act.copy(pT[:, h, j, i0:T], BANK_T(j)[:, i0:T]).then_inc(turned_copied, 1)

            def body(n, last):
                for h in range(HG):
                    for i in range(NB):
                        exp(n, h, i)
                        if h > 0:
                            copy(n, h - 1, i)
                if not last:
                    evacuate(n + 1)
                for j in range(NB):
                    copy(n, HG - 1, j)
                act.wait_ge(pv_ready, n + 1)
                wait_past(act, o_normed, n)
                act.copy(o_sb[:], BANK_A).then_inc(o_copied, 1)

            evacuate(0)
            peeled(body)(act)

        @block.vector
        def _(ve):
            hi0 = NG if rel else 0

            def stacks(n):
                hb = hi0 + NPROJ * n
                sb_ = NPROJ * n
                ve.wait_ge(q_scaled, sb_ + 1)
                wait_past(ve, scores_ready, HG * NB * n)
                ve.tensor_copy(q_hi[:], qs[:]).then_inc(hi_copied, 1)
                ve.wait_ge(hi_copied, hb + 1)
                for h in range(HG):
                    r = slice(h * QW, (h + 1) * QW)
                    ve.scalar_tensor_tensor(out=qz[r, h, :], in0=q_hi[r, :].bitcast(F32), scalar=consts["neg_lo_q"][r, :],
                                            in1=qs[r, :], op0=ALU.mult, op1=ALU.add).then_inc(stacked, 1)
                if rel:
                    ve.wait_ge(q_scaled, sb_ + 2)
                    ve.tensor_copy(a_hi[:], as_[:]).then_inc(hi_copied, 1)
                    ve.wait_ge(hi_copied, hb + 2)
                    ve.scalar_tensor_tensor(out=ast[:], in0=a_hi[:].bitcast(F32), scalar=consts["neg_lo_q"],
                                            in1=as_[:], op0=ALU.mult, op1=ALU.add).then_inc(stacked, 1)
                ve.wait_ge(q_scaled, sb_ + NPROJ)
                ve.tensor_copy(k_hi[:], ks[:]).then_inc(hi_copied, 1)
                ve.wait_ge(hi_copied, hb + NPROJ)
                ve.scalar_tensor_tensor(out=kst[:], in0=k_hi[:].bitcast(F32), scalar=consts["neg_lo_k"],
                                        in1=ks[:], op0=ALU.mult, op1=ALU.add).then_inc(stacked, 1)

            def head(n, h):
                base = HG * NB * n + NB * h
                if rel:
                    ve.wait_ge(g_ready, HG * n + h + 1)
                    wait_past(ve, g_summed, HG * n + h)
                    ve.tensor_tensor(rot1[:], BANK_A, consts["cos"], ALU.mult).then_inc(rotated, 1)
                    ve.tensor_tensor(rot2[:], BANK_B, consts["sin"], ALU.mult).then_inc(rotated, 1)
                for i in range(NB):
                    w = T if rel else (i + 1) * P
                    ve.wait_ge(scores_ready, base + i + 1)
                    if rel:
                        dw = min(DIAG, T - i * P)
                        d = slice(i * P, i * P + dw)
                        both = ps[:, 4 + i % 2, 0:2 * DIAG].rearrange("p (k m) -> p k m", k=2)
                        wait_past(ve, diag_added, base + i)
                        ve.tensor_tensor(diag[:, :, 0:dw], both[:, :, 0:dw], consts["tri"][:, :, 0:dw], ALU.mult).then_inc(diag_masked, 1)
                        ve.wait_ge(diag_masked, base + i + 1)
                        ve.tensor_tensor(dsum[:, 0:dw], diag[:, 0, 0:dw], diag[:, 1, 0:dw], ALU.add).then_inc(diag_summed, 1)
                        ve.wait_ge(diag_summed, base + i + 1)
                        ve.tensor_tensor(S(i)[:, d], S(i)[:, d], dsum[:, 0:dw], ALU.add).then_inc(diag_added, 1)
                        ve.wait_ge(diag_added, base + i + 1)
                    if i == 0:
                        wait_past(ve, exp_ready, base + NB - HG * NB)
                    ve.tensor_reduce(negmax[:, h, i:i + 1], S(i)[:, 0:w], AX_X, ALU.max, negate=True).then_inc(max_ready, 1)

            def tail(n):
                ve.wait_ge(sums_ready, n + 1)
                ve.reciprocal(recip[:], BANK_B).then_inc(recip_ready, 1)
                ve.wait_ge(recip_ready, n + 1)
                ve.tensor_tensor(o_norm[:], o_sb[:], recip[:], ALU.mult).then_inc(o_normed, 1)
                ve.wait_ge(wo_done, n + 1)
                s = bass.ds((n // NG) * T, T)
                wait_past(ve, x_added, n)
                ve.scalar_tensor_tensor(out=xT[:, s], in0=BANK_A, scalar=gate[:, bass.ds(n // NG, 1)],
                                        in1=xT[:, s], op0=ALU.mult, op1=ALU.add).then_inc(x_added, 1)

            def body(n, last):
                for h in range(HG):
                    head(n, h)
                if not last:
                    stacks(n + 1)
                tail(n)

            stacks(0)
            peeled(body)(ve)

        @block.gpsimd
        def _(pool):
            if not rel:
                return

            def body(n, last):
                for h in range(HG):
                    base = HG * NB * n + NB * h
                    pool.wait_ge(rotated, 2 * (HG * n + h + 1))
                    wait_past(pool, scores_ready, base)
                    pool.tensor_tensor(gT[:, 0:T], rot1[:], rot2[:], ALU.add).then_inc(g_summed, 1)

            peeled(body)(pool)


def add_router(nc, cfg, hT, CT, consts, dram):
    E, NT, name = cfg.E, NTOK // P, "r1" if cfg.rel else "r0"
    G, GE = 8, 8
    BIG = 3e38
    with ExitStack() as ctx:
        sb = lambda n, s, d=F32: ctx.enter_context(nc.sbuf_tensor(f"{name}_{n}", s, d))
        sem = lambda n: nc.alloc_semaphore(f"{name}_{n}")
        lg_ps = ctx.enter_context(nc.psum_tensor(f"{name}_lg", [P, NT, 64], F32))
        tp_ps = ctx.enter_context(nc.psum_tensor(f"{name}_tp", [P, B, T], F32))
        gw, bias = sb("gw", [P, E]), sb("bias", [P, E])
        score, biased, rep = sb("score", [P, NT, E]), sb("biased", [P, NT, E]), sb("rep", [P, NT, E])
        v8, red, rcp = sb("v8", [P, NT, 8]), sb("red", [P, NT]), sb("rcp", [P, NT])
        sel, comb = sb("sel", [P, NT, E]), sb("comb", [P, NT, E])
        stack = sb("stack", [P, NT, P], F32R)
        if cfg.rel:
            masked = sb("masked", [P, NT, E])
            gmask = sb("gmask", [P, NT, G], U32)
            emask = sb("emask", [P, NT * G, GE], U32)
            hi1, lo1, t1, t2 = (sb(n, [P, NT * G, 4]) for n in ("hi1", "lo1", "t1", "t2"))
            gs, grep = sb("gs", [P, NT, G]), sb("grep", [P, NT, G])
        loaded, logits_ready, act_ready, step = sem("ld"), sem("lg"), sem("act"), sem("st")
        stacked, turned, in_ready = sem("stk"), sem("tr"), sem("in")
        block = ctx.enter_context(nc.Block())
        logits = lg_ps[:, :, 0:E]

        def over_experts(a):
            return a.unsqueeze(2).broadcast_to([P, NT, E])

        @block.sync
        def _(sp):
            sp.dma_start(gw[:], dram["gate"]).then_inc(loaded, 16)
            sp.dma_start(bias[:], dram["bias"]).then_inc(loaded, 16)

        @block.gpsimd
        def _(pool):
            pool.memset(stack[:].bitcast(F32), 0.0).then_inc(in_ready, 1)
            if cfg.rel:
                pool.memset(masked[:], 0.0).then_inc(in_ready, 1)

        @block.tensor
        def _(pe):
            pe.wait_ge(loaded, 32)
            for t in range(NT):
                mm = pe.matmul(lg_ps[:, t, 0:E], hT[:, t * P:(t + 1) * P], gw[:], start=True, stop=True)
            mm.then_inc(logits_ready, 1)
            pe.wait_ge(stacked, 2)
            for t in range(NT):
                tr = pe.transpose(tp_ps[:, t // NB, (t % NB) * P:(t % NB + 1) * P], stack[:, t, :].bitcast(F32), consts["ident"])
                if t % NB == NB - 1:
                    tr.then_inc(turned, 1)

        @block.scalar
        def _(act):
            if cfg.rel:
                act.wait_ge(logits_ready, 1)
                act.activation(score[:], logits, ACT.Sigmoid).then_inc(act_ready, 1)
            else:
                act.wait_ge(step, 2)
                act.activation(rep[:], biased[:], ACT.Exp).then_inc(act_ready, 1)
            for b in range(B):
                act.wait_ge(turned, b + 1)
                act.copy(CT[:, b * T:(b + 1) * T], tp_ps[:, b, :])

        @block.vector
        def _(ve):
            done = [0]

            def chain(ins):
                done[0] += 1
                ins.then_inc(step, 1)
                ve.wait_ge(step, done[0])

            ve.wait_ge(loaded, 32)
            ve.wait_ge(in_ready, 1 + cfg.rel)
            if not cfg.rel:
                ve.wait_ge(logits_ready, 1)
                chain(ve.tensor_reduce(red[:], logits, AX_X, ALU.max))
                chain(ve.tensor_tensor(biased[:], logits, over_experts(red[:]), ALU.subtract))
                ve.wait_ge(act_ready, 1)
                chain(ve.reduce_sum(red[:], rep[:], AX_X))
                chain(ve.reciprocal(rcp[:], red[:]))
                chain(ve.tensor_tensor(score[:], rep[:], over_experts(rcp[:]), ALU.mult))
            else:
                ve.wait_ge(act_ready, 1)
            bias_all = bias[:].unsqueeze(1).broadcast_to([P, NT, E])
            chain(ve.tensor_tensor(biased[:], score[:], bias_all, ALU.add))

            def pick_top(out, values, k):
                for t in range(NT):
                    ins = ve.max(v8[:, t, :], values[:, t, :])
                chain(ins)
                if k < 8:
                    chain(ve.memset(v8[:, :, k:8], BIG))
                for t in range(NT):
                    ins = ve.match_replace(out[:, t, :], v8[:, t, :], values[:, t, :], -BIG)
                chain(ins)

            if not cfg.rel:
                pick_top(rep[:], biased[:], 2)
                chain(ve.tensor_scalar(sel[:], rep[:], -1e38, None, ALU.is_le))
                chain(ve.tensor_tensor(comb[:], score[:], sel[:], ALU.mult))
            else:
                def pairs(a, n):
                    v = a.rearrange("p g (n two) -> p g n two", two=2)
                    return v[:, :, :, 0], v[:, :, :, 1]

                v = biased[:].rearrange("p t (g e) -> p (t g) e", e=GE)
                a, b_ = pairs(v, 4)
                chain(ve.tensor_tensor(hi1[:], a, b_, ALU.max))
                chain(ve.tensor_tensor(lo1[:], a, b_, ALU.min))
                w = 4
                while w > 1:
                    ha, hb = pairs(hi1[:, :, 0:w], w // 2)
                    la, lb = pairs(lo1[:, :, 0:w], w // 2)
                    u = w // 2
                    chain(ve.tensor_tensor(t1[:, :, 0:u], ha, hb, ALU.min))
                    chain(ve.tensor_tensor(t2[:, :, 0:u], la, lb, ALU.max))
                    chain(ve.tensor_tensor(t2[:, :, 0:u], t1[:, :, 0:u], t2[:, :, 0:u], ALU.max))
                    chain(ve.tensor_tensor(t1[:, :, 0:u], ha, hb, ALU.max))
                    chain(ve.tensor_copy(hi1[:, :, 0:u], t1[:, :, 0:u]))
                    chain(ve.tensor_copy(lo1[:, :, 0:u], t2[:, :, 0:u]))
                    w = u
                chain(ve.tensor_tensor(gs[:].rearrange("p t g -> p (t g)"), hi1[:, :, 0], lo1[:, :, 0], ALU.add))
                pick_top(grep[:], gs[:], 4)
                chain(ve.tensor_scalar(gmask[:], grep[:], -1e38, None, ALU.is_le))
                chain(ve.tensor_copy(emask[:], gmask[:].rearrange("p t g -> p (t g)").unsqueeze(2).broadcast_to([P, NT * G, GE])))
                chain(ve.copy_predicated(masked[:].rearrange("p t (g e) -> p (t g) e", e=GE), emask[:], v))
                pick_top(rep[:], masked[:], 8)
                chain(ve.tensor_scalar(sel[:], rep[:], -1e38, None, ALU.is_le))
                chain(ve.tensor_tensor(sel[:], score[:], sel[:], ALU.mult))
                chain(ve.reduce_sum(red[:], sel[:], AX_X))
                chain(ve.tensor_scalar(red[:], red[:], 1e-20, None, ALU.add))
                chain(ve.reciprocal(rcp[:], red[:]))
                chain(ve.tensor_scalar(rcp[:], rcp[:], 2.5, None, ALU.mult))
                chain(ve.tensor_tensor(comb[:], sel[:], over_experts(rcp[:]), ALU.mult))
            ve.tensor_copy(stack[:, :, 0:E], comb[:]).then_inc(stacked, 1)
            ve.wait_ge(stacked, 1)
            ve.tensor_tensor(stack[:, :, 64:64 + E], comb[:], stack[:, :, 0:E].bitcast(F32), ALU.subtract).then_inc(stacked, 1)


def add_moe(nc, cfg, xT, h_hi, h_lo, CT, gate, dram):
    up, name = cfg.up, "m1" if cfg.rel else "m0"
    U = cfg.units + 2
    STEPS = U // 2
    SEL, DOWN = up, up + 1
    NSH = 2 * B
    with ExitStack() as ctx:
        sb = lambda n, s, d=F32: ctx.enter_context(nc.sbuf_tensor(f"{name}_{n}", s, d))
        sem = lambda n: nc.alloc_semaphore(f"{name}_{n}")
        ps = ctx.enter_context(nc.psum_tensor(f"{name}_ps", [P, 8, T], F32))
        w = [sb(f"w{q}", [P, up + 2, P]) for q in range(2)]
        w_hi = [sb(f"whi{q}", [P, up + 1, P], F32R) for q in range(2)]
        w_lo = [sb(f"wlo{q}", [P, up, P], F32R) for q in range(2)]
        acts = sb("acts", [P, 2, T])
        scaled = sb("scaled", [P, 2, T])
        hidden = sb("hidden", [P, 2, T])
        w_loaded = [sem("wl0"), sem("wl1")]
        w_rounded, w_split = sem("wr"), sem("ws")
        up_ready, comb_ready, act_ready = sem("up"), sem("cb"), sem("act")
        scaled_ready, hidden_ready, down_done, added = sem("sc"), sem("hid"), sem("dn"), sem("add")
        A = lambda m: ps[:, 4 + m % 2, :]
        Bk = ps[:, 6, :]
        C = lambda m: ps[:, 6 + m % 2, :] if up == 1 else ps[:, 7, :]
        block = ctx.enter_context(nc.Block())

        def steps(eng, body):
            body(0, False)
            with eng.Fori(1, STEPS - 1) as k:
                body(k, False)
            body(STEPS - 1, True)

        @block.sync
        def _(sp):
            def body(k, last):
                for q in range(2):
                    u = 2 * k + q
                    wait_past(sp, w_loaded[q], 16 * k)
                    wait_past(sp, down_done, B * u - B)
                    sp.dma_start(w[q][:], dram["units"][bass.ds(u, 1)].rearrange("o p (k m) -> p (o k) m", k=up + 2)).then_inc(w_loaded[q], 16)

            steps(sp, body)

        @block.tensor
        def _(pe):
            def down(m, q, b, first):
                pe.wait_ge(hidden_ready, m + 1)
                pe.matmul(ps[:, b, :], w[q][:, DOWN, :], hidden[:, b % 2, :], start=first, stop=False,
                          skip_group_check=True).then_inc(down_done, 1)

            def body(k, last):
                shared = isinstance(k, int) and k == 0
                for q in range(2):
                    u = 2 * k + q
                    pe.wait_ge(w_split, u + 1)
                    for b in range(B):
                        m = B * u + b
                        tok = slice(b * T, (b + 1) * T)
                        for a in range(up):
                            bank = A(b) if a == 0 else Bk
                            if a == 0:
                                wait_past(pe, act_ready, m - 1)
                            else:
                                wait_past(pe, hidden_ready, m)
                            pe.matmul(bank, w_hi[q][:, a, :], h_hi[:, tok], start=True, stop=False)
                            pe.matmul(bank, w_hi[q][:, a, :], h_lo[:, tok], start=False, stop=False)
                            mm = pe.matmul(bank, w_lo[q][:, a, :], h_hi[:, tok], start=False, stop=True)
                        mm.then_inc(up_ready, 1)
                        if not shared:
                            pe.wait_ge(hidden_ready, m - 1 if up == 1 else m)
                            pe.matmul(C(b), w_hi[q][:, SEL, :], CT[:, tok], start=True, stop=True).then_inc(comb_ready, 1)
                        if shared and m == 0:
                            continue
                        pb, pq = (b - 1, q) if b else (B - 1, 1 - q)
                        down(m - 1, pq, pb, first=shared and m - 1 < B)
                if last:
                    down(B * U - 1, 1, B - 1, False)

            steps(pe, body)

        @block.scalar
        def _(act):
            def body(k, last):
                for q in range(2):
                    for b in range(B):
                        m = B * (2 * k + q) + b
                        act.wait_ge(up_ready, m + 1)
                        wait_past(act, hidden_ready, m - 1)
                        act.activation(acts[:, b % 2, :], A(b), ACT.Relu if up == 1 else ACT.Silu).then_inc(act_ready, 1)

            steps(act, body)

        def split(ve, u, k, q):
            ve.wait_ge(w_loaded[q], 16 * (k + 1))
            wait_past(ve, up_ready, B * (u - 1))
            wait_past(ve, hidden_ready, B * (u - 1))
            ve.tensor_copy(w_hi[q][:], w[q][:, 0:up + 1, :]).then_inc(w_rounded, 1)
            ve.wait_ge(w_rounded, u + 1)
            ve.tensor_tensor(w_lo[q][:], w[q][:, 0:up, :], w_hi[q][:, 0:up, :].bitcast(F32), ALU.subtract).then_inc(w_split, 1)

        @block.vector
        def _(ve):
            split(ve, 0, 0, 0)

            def body(k, last):
                shared = isinstance(k, int) and k == 0
                for q in range(2):
                    u = 2 * k + q
                    for b in range(B):
                        m = B * u + b
                        if b == 3 and not (last and q == 1):
                            split(ve, u + 1, k + q, 1 - q)
                        if up == 2:
                            ve.wait_ge(act_ready, m + 1)
                            wait_past(ve, down_done, m - 1)
                            if shared:
                                ve.tensor_tensor(hidden[:, b % 2, :], Bk, acts[:, b % 2, :], ALU.mult).then_inc(hidden_ready, 1)
                                continue
                            ve.tensor_tensor(scaled[:, b % 2, :], Bk, acts[:, b % 2, :], ALU.mult).then_inc(scaled_ready, 1)
                            ve.wait_ge(comb_ready, m + 1 - NSH)
                            ve.wait_ge(scaled_ready, m + 1 - NSH)
                            ve.tensor_tensor(hidden[:, b % 2, :], C(b), scaled[:, b % 2, :], ALU.mult).then_inc(hidden_ready, 1)
                        elif not shared:
                            ve.wait_ge(act_ready, m + 1)
                            ve.wait_ge(comb_ready, m + 1 - NSH)
                            ve.wait_ge(hidden_ready, m - 1)
                            ve.tensor_tensor(scaled[:, b % 2, :], C(b), acts[:, b % 2, :], ALU.mult).then_inc(scaled_ready, 1)

            steps(ve, body)
            for b in range(B):
                ve.wait_ge(down_done, B * (U - 1) + b + 1)
                s = slice(b * T, (b + 1) * T)
                ve.scalar_tensor_tensor(out=xT[:, s], in0=ps[:, b, :], scalar=gate[:, b:b + 1], in1=xT[:, s],
                                        op0=ALU.mult, op1=ALU.add).then_inc(added, 1)

        @block.gpsimd
        def _(pool):
            if up == 2:
                return

            def body(k, last):
                shared = isinstance(k, int) and k == 0
                for q in range(2):
                    for b in range(B):
                        m = B * (2 * k + q) + b
                        wait_past(pool, down_done, m - 1)
                        pool.wait_ge(act_ready, m + 1)
                        other = acts if shared else scaled
                        if not shared:
                            pool.wait_ge(scaled_ready, m + 1 - NSH)
                        pool.tensor_tensor(hidden[:, b % 2, :], acts[:, b % 2, :], other[:, b % 2, :], ALU.mult).then_inc(hidden_ready, 1)

            steps(pool, body)


N_CONST = 3 * P + 2 * DIAG + 4 * T + 2


def build_program(nc, a, out, upto=99):
    with ExitStack() as ctx:
        sb = lambda n, s, d=F32: ctx.enter_context(nc.sbuf_tensor(n, s, d))
        xT, hT = sb("xT", [P, NTOK]), sb("hT", [P, NTOK])
        const = sb("const", [P, N_CONST])
        bf = sb("const_bf", [P, 2, P], BF16)
        mods = [sb(f"mod{k}", [P, 6, B]) for k in range(2)]
        mean_w, eps_col = sb("mean_w", [P, P]), sb("eps", [P, 1])
        wv, gb, bv = [sb(f"wv{k}", [P, D]) for k in range(2)], sb("ln_gb", [P, 2]), sb("bv", [P, D])
        load_done, out_done = (nc.alloc_semaphore(n) for n in ("load_done", "out_done"))

        consts, at = {}, 0
        for key, n in (("ident", P), ("causal_f", P), ("pick", P), ("tri", 2 * DIAG), ("pe", 2 * T), ("cos", T), ("sin", T),
                       ("neg_lo_q", 1), ("neg_lo_k", 1)):
            consts[key] = const[:, at:at + n]
            at += n
        consts["tri"] = consts["tri"].rearrange("p (k m) -> p k m", k=2)
        consts["ident_bf"], consts["causal"] = bf[:, 0, :], bf[:, 1, :]

        with nc.Block() as block:
            @block.sync
            def _(sp):
                for dst, src in ((xT[:], a["xT"]), (const[:, 0:at], a["const"]), (wv[0][:], a["wv0"]), (wv[1][:], a["wv1"]),
                                 (gb[:], a["ln_gb"]), (bv[:], a["bv"])):
                    sp.dma_start(dst, src).then_inc(load_done, 16)
                sp.wait_ge(load_done, 96)

            @block.vector
            def _(ve):
                ve.memset(mean_w[:], 1.0 / D)
                ve.memset(eps_col[:], LN_EPS)
                ve.wait_ge(load_done, 96)
                ve.tensor_copy(bf[:, 0, :], consts["ident"])
                ve.tensor_copy(bf[:, 1, :], consts["causal_f"])

        counts = {}
        add_modulation(nc, [(a["c0"], a["wmod0"], mods[0]), (a["c1"], a["wmod1"], mods[1])])

        for k, cfg in enumerate((Cfg(False), Cfg(True))):
            mod = mods[k]
            shift = lambda j, mod=mod: (lambda b: mod[:, j, b:b + 1])
            if upto < 4 * k + 1:
                break
            with nc.sbuf_tensor(f"vall{k}", [P, B * NB, H, QW], F32) as vall:
                with nc.Block() as block:
                    @block.gpsimd
                    def _(pool):
                        pool.memset(vall[:, :, :, 0:DH + 1], 1.0)
                        pool.memset(vall[:, :, :, DH + 1:QW], 0.0)
                if cfg.rel:
                    add_layernorm(nc, f"ln{k}m", xT, hT, shift(1), shift(0), mean_w, eps_col, counts=counts)
                    add_layernorm(nc, f"ln{k}a", hT, hT, lambda b: gb[:, 0:1], lambda b: gb[:, 1:2], mean_w, eps_col, wv=wv[k], bv=bv, vall=vall, counts=counts)
                else:
                    add_layernorm(nc, f"ln{k}a", xT, hT, shift(1), shift(0), mean_w, eps_col, wv=wv[k], vall=vall, counts=counts)
                if upto < 4 * k + 2:
                    break
                add_attention(nc, cfg, xT, hT, vall, mod[:, 2, :], consts,
                              {n: a.get(f"{n}{k}") for n in ("wqk", "wo", "wp", "cols")})
            if upto < 4 * k + 3:
                break
            with nc.sbuf_tensor(f"hhi{k}", [P, NTOK], F32R) as h_hi, nc.sbuf_tensor(f"hlo{k}", [P, NTOK], F32R) as h_lo, \
                    nc.sbuf_tensor(f"CT{k}", [P, NTOK], F32R) as CT:
                add_layernorm(nc, f"ln{k}f", xT, hT, shift(4), shift(3), mean_w, eps_col, dst_hi=h_hi, dst_lo=h_lo, counts=counts)
                add_router(nc, cfg, hT, CT, consts, {n: a[f"{n}{k}"] for n in ("gate", "bias")})
                if upto < 4 * k + 4:
                    break
                add_moe(nc, cfg, xT, h_hi, h_lo, CT, mod[:, 5, :], {"units": a[f"units{k}"]})

        with nc.Block() as block:
            @block.sync
            def _(sp):
                res = hT if upto in (1, 5) else xT
                sp.dma_start(out, res[:]).then_inc(out_done, 16)
                sp.wait_ge(out_done, 16)


def constants():
    ident = np.eye(P)
    i, j = np.arange(P)[:, None], np.arange(P)[None, :]
    causal = np.where(j > i, NEG, 0.0)
    pick = ((i == (j // QW) * QW + DH)).astype(float)
    jd = np.arange(DIAG)[None, :]
    tri = np.concatenate([(jd <= i), (jd >= i + 2)], 1).astype(float)
    div = np.exp(np.arange(0, D, 2, dtype=np.float32) * np.float32(-np.log(10000.0) / D)).astype(np.float64)
    w = np.repeat(div, 2)[:, None]
    odd = (np.arange(D) % 2)[:, None]
    x = np.concatenate([np.arange(T), T + np.arange(T)])[None, :]
    pe = np.where(odd == 1, np.cos(w * x), np.sin(w * x))
    r = np.arange(1, T + 1)[None, :]
    cos, sin = np.cos(w * r), np.sin(w * r) * np.where(odd == 1, -1.0, 1.0)
    row = np.arange(P)[:, None] % QW // DH
    return np.concatenate([ident, causal, pick, tri, pe, cos, sin, -1.0 * (row == 1), -1.0 * (row == 2)], 1).astype(np.float32)


def stacked_columns(w):
    w = w.reshape(w.shape[0], NG, HG, 1, DH)
    z = np.zeros_like(w)
    return np.concatenate([w, w, w, z], 3).reshape(w.shape[0], NG, P).transpose(1, 0, 2)


def selectors(units, up):
    s = np.zeros((units + 2, P, P), np.float32)
    for u in range(units):
        for m in range(P):
            e = u // 2 if up == 2 else 2 * u + m // 64
            s[u + 2, e, m] = s[u + 2, 64 + e, m] = 1.0
    return s


def pack_units(ups, sel, down):
    return np.ascontiguousarray(np.concatenate([*ups, sel, down], 2))


def lay_out(d):
    f = {k: np.asarray(v) for k, v in d.items()}
    a = {"xT": f["L0_attn_x"].reshape(NTOK, D).T, "const": constants(), "ln_gb": np.stack([f["L1_attn_ln_g"], f["L1_attn_ln_b"]], 1)}
    for k in range(2):
        p = f"L{k}_attn_"
        a[f"c{k}"], a[f"wmod{k}"] = f[f"L{k}_c"].T, f[f"L{k}_wmod"]
        a[f"wv{k}"] = f[p + "Wv"]
        a[f"wqk{k}"] = np.concatenate([stacked_columns(f[p + "Wq"]), stacked_columns(f[p + "Wk"])], 2)
        wo = f[p + "Wo"].reshape(NG, HG, DH, D)
        a[f"wo{k}"] = np.concatenate([wo, np.zeros((NG, HG, QW - DH, D), np.float32)], 2).reshape(NG, P, D)
    p = "L1_attn_"
    wp = f[p + "Wp"]
    swapped = wp.reshape(D // 2, 2, D)[:, ::-1].reshape(D, D)
    both = np.stack([stacked_columns(wp), stacked_columns(swapped)])
    both = both.reshape(2, NG, D, HG, QW)
    z = np.zeros((NG, HG, QW, HG, 2, D), np.float32)
    for h in range(HG):
        z[:, h, :, h] = both[:, :, :, h].transpose(1, 3, 0, 2)
    a["wp1"] = z.reshape(NG, P, HG * 2 * D)
    col = lambda v: stacked_columns(v.reshape(1, D))[:, 0, :].T
    a["cols1"] = np.stack([col(f[p + "bq"]), col(f[p + "u_bias"]), col(f[p + "v_bias"]), col(f[p + "bk"]),
                           np.repeat(f[p + "bo"][:, None], NG, 1)], 1)
    a["bv"] = np.broadcast_to(f[p + "bv"], (P, D))
    a["gate0"], a["gate1"] = f["L0_ffn_gate_w"].T, f["L1_ffn_router_w"].T
    a["bias0"] = np.broadcast_to(f["L0_ffn_gate_bias"], (P, 8))
    a["bias1"] = np.broadcast_to(f["L1_ffn_correction_bias"], (P, 64))
    halves = lambda shared, w: np.concatenate([shared[None], w]).reshape(-1, P, D)
    w1, w3 = (halves(f[f"L0_ffn_s{n}"], f[f"L0_ffn_{n}"]).transpose(0, 2, 1) for n in ("w1", "w3"))
    w2 = np.concatenate([f["L0_ffn_sw2"][None], f["L0_ffn_w2"]]).transpose(0, 2, 1).reshape(-1, P, D)
    a["units0"] = pack_units([w1, w3], selectors(16, 2), w2)
    up = f["L1_ffn_up_w"].reshape(32, 2, D, 64).transpose(0, 2, 1, 3).reshape(32, D, P)
    sup = f["L1_ffn_shared_up_w"].reshape(D, 2, P).transpose(1, 0, 2)
    down = f["L1_ffn_down_w"].reshape(32, P, D)
    sdown = f["L1_ffn_shared_down_w"].reshape(2, P, D)
    a["units1"] = pack_units([np.concatenate([sup, up])], selectors(32, 1), np.concatenate([sdown, down]))
    return {k: np.ascontiguousarray(v) for k, v in a.items()}


def kernel(**inputs):
    import concourse.bacc as bacc
    from concourse.bass_utils import run_bass_kernel_spmd

    nc = bacc.Bacc("TRN2", target_bir_lowering=False, num_devices=1)
    arrays = lay_out(inputs)
    aps = {k: nc.dram_tensor(f"in_{k}", v.shape, mybir.dt.from_np(v.dtype), kind="ExternalInput").ap() for k, v in arrays.items()}
    out = nc.dram_tensor("out_xT", (P, NTOK), F32, kind="ExternalOutput").ap()
    build_program(nc, aps, out)
    r = run_bass_kernel_spmd(nc, [{f"in_{k}": v for k, v in arrays.items()}], core_ids=[0])
    return np.ascontiguousarray(r.results[0]["out_xT"].T).reshape(B, T, D)
```

```python
from contextlib import ExitStack

import numpy as np

import concourse.bass as bass
from concourse import mybir

P = 128
F32 = mybir.dt.float32
F32R = mybir.dt.float32r
BF16 = mybir.dt.bfloat16
U32 = mybir.dt.uint32
ALU = mybir.AluOpType
ACT = mybir.ActivationFunctionType
AX_X = mybir.AxisListType.X

B, T, D = 4, 512, 128
NTOK = B * T
H, DH = 16, 8
HG = 4
NG = H // HG
NIT = B * NG
NB = T // P
DIAG = P + 1
QW = 32
LN_EPS = 1e-5
NEG = -1e30


class Cfg:

    def __init__(self, rel):
        self.rel = rel
        self.scale = float(DH) ** -0.5
        self.E = 64 if rel else 8
        self.up = 1 if rel else 2
        self.units = 32 if rel else 16


def wait_past(eng, sem, value):
    if isinstance(value, int) and value <= 0:
        return
    eng.wait_ge(sem, value)


def add_layernorm(nc, name, src, dst, mul, add, ones, eps, dst_hi=None, dst_lo=None, wv=None, bv=None, vall=None, counts=None):
    with ExitStack() as ctx:
        sb = lambda n, s, d=F32: ctx.enter_context(nc.sbuf_tensor(f"{name}_{n}", s, d))
        mean_ps = ctx.enter_context(nc.psum_tensor(f"{name}_mean", [P, B, T], F32))
        var_ps = ctx.enter_context(nc.psum_tensor(f"{name}_var", [P, B, T], F32))
        xc = sb("xc", [P, B, T])
        sq = sb("sq", [P, B, T])
        std, rstd = sb("std", [P, B, T]), sb("rstd", [P, B, T])
        norm = sb("norm", [P, B, T])
        names = ("mean_ready", "centered", "squared", "var_ready", "std_ready", "rstd_ready", "norm_ready", "out_ready")
        names += (("hi_ready", "lo_ready") if dst_hi is not None else ()) + (("v_ready",) if wv is not None else ())
        sem, base = {}, {}
        for n in names:
            sem[n], base[n] = counts.setdefault(n, (None, 0))
            if sem[n] is None:
                sem[n] = nc.alloc_semaphore(f"ln_{n}")
            counts[n] = (sem[n], base[n] + B)

        def wait(eng, n, value):
            eng.wait_ge(sem[n], base[n] + value)

        block = ctx.enter_context(nc.Block())

        def v_of(b, t):
            return mean_ps[:, b, t * P:(t + 1) * P].rearrange("p (h d) -> p h d", d=DH)

        @block.tensor
        def _(pe):
            for b in range(B):
                pe.matmul(mean_ps[:, b, :], ones[:], src[:, b * T:(b + 1) * T], start=True, stop=True).then_inc(sem["mean_ready"], 1)
            for b in range(B):
                wait(pe, "squared", b + 1)
                pe.matmul(var_ps[:, b, :], ones[:], sq[:, b, :], start=True, stop=True).then_inc(sem["var_ready"], 1)
            if wv is not None:
                for b in range(B):
                    wait(pe, "out_ready", b + 1)
                    wait(pe, "centered", b + 1)
                    for t in range(NB):
                        lo = b * T + t * P
                        mm = pe.matmul(mean_ps[:, b, t * P:(t + 1) * P], dst[:, lo:lo + P], wv[:], start=True, stop=True)
                    mm.then_inc(sem["v_ready"], 1)

        @block.scalar
        def _(act):
            for b in range(B):
                wait(act, "centered", b + 1)
                act.activation(sq[:, b, :], xc[:, b, :], ACT.Square).then_inc(sem["squared"], 1)
            for b in range(B):
                wait(act, "var_ready", b + 1)
                act.activation(std[:, b, :], var_ps[:, b, :], ACT.Sqrt, bias=eps[:, 0:1]).then_inc(sem["std_ready"], 1)
            if wv is not None and bv is None:
                for b in range(B):
                    wait(act, "v_ready", b + 1)
                    for t in range(NB):
                        act.copy(vall[:, b * NB + t, :, 0:DH], v_of(b, t))

        @block.vector
        def _(ve):
            for b in range(B):
                wait(ve, "mean_ready", b + 1)
                ve.tensor_tensor(xc[:, b, :], src[:, b * T:(b + 1) * T], mean_ps[:, b, :], ALU.subtract).then_inc(sem["centered"], 1)
            for b in range(B):
                wait(ve, "std_ready", b + 1)
                ve.reciprocal(rstd[:, b, :], std[:, b, :]).then_inc(sem["rstd_ready"], 1)
                wait(ve, "rstd_ready", b + 1)
                ve.tensor_tensor(norm[:, b, :], xc[:, b, :], rstd[:, b, :], ALU.mult).then_inc(sem["norm_ready"], 1)
                wait(ve, "norm_ready", b + 1)
                ve.tensor_scalar(dst[:, b * T:(b + 1) * T], norm[:, b, :], mul(b), add(b), ALU.mult, ALU.add).then_inc(sem["out_ready"], 1)
                if dst_hi is not None:
                    wait(ve, "out_ready", b + 1)
                    ve.tensor_copy(dst_hi[:, b * T:(b + 1) * T], dst[:, b * T:(b + 1) * T]).then_inc(sem["hi_ready"], 1)
            if bv is not None:
                for b in range(B):
                    wait(ve, "v_ready", b + 1)
                    for t in range(NB):
                        ve.tensor_tensor(vall[:, b * NB + t, :, 0:DH], v_of(b, t), bv[:].rearrange("p (h d) -> p h d", d=DH), ALU.add)

        @block.gpsimd
        def _(pool):
            if dst_lo is not None:
                for b in range(B):
                    wait(pool, "hi_ready", b + 1)
                    s = slice(b * T, (b + 1) * T)
                    pool.tensor_tensor(dst_lo[:, s], dst[:, s], dst_hi[:, s].bitcast(F32), ALU.subtract).then_inc(sem["lo_ready"], 1)


def add_modulation(nc, layers):
    with ExitStack() as ctx:
        sem = lambda n: nc.alloc_semaphore(f"mod_{n}")
        loaded, silu_ready, made, copied, step = sem("ld"), sem("silu"), sem("mm"), sem("cp"), sem("step")
        tiles = []
        for k, (cT, wmod, mod) in enumerate(layers):
            tiles.append((
                ctx.enter_context(nc.sbuf_tensor(f"mod_c{k}", [P, B], F32)),
                ctx.enter_context(nc.sbuf_tensor(f"mod_s{k}", [P, B], F32)),
                ctx.enter_context(nc.sbuf_tensor(f"mod_w{k}", [P, 6 * D], F32)),
                ctx.enter_context(nc.sbuf_tensor(f"mod_sg{k}", [P, 2, B], F32)),
                ctx.enter_context(nc.sbuf_tensor(f"mod_mg{k}", [P, 2, B], F32)),
                ctx.enter_context(nc.psum_tensor(f"mod_p{k}", [P, 6, B], F32)),
            ))
        n = len(layers)
        block = ctx.enter_context(nc.Block())

        @block.sync
        def _(sp):
            for (cT, wmod, _), t in zip(layers, tiles):
                sp.dma_start(t[0][:], cT).then_inc(loaded, 16)
                sp.dma_start(t[2][:], wmod).then_inc(loaded, 16)

        @block.scalar
        def _(act):
            act.wait_ge(loaded, 32 * n)
            for t in tiles:
                act.activation(t[1][:], t[0][:], ACT.Silu).then_inc(silu_ready, 1)

        @block.tensor
        def _(pe):
            pe.wait_ge(silu_ready, n)
            for t in tiles:
                for k in range(6):
                    mm = pe.matmul(t[5][:, k, :], t[2][:, k * D:(k + 1) * D], t[1][:], start=True, stop=True)
                mm.then_inc(made, 1)

        @block.vector
        def _(ve):
            for k, ((_, _, mod), t) in enumerate(zip(layers, tiles)):
                ve.wait_ge(made, k + 1)
                ve.tensor_copy(mod[:], t[5][:]).then_inc(copied, 1)
                ve.wait_ge(copied, k + 1)
                sg, mg = t[3], t[4]
                gates = mod[:, 2::3, :]
                gains = mod[:, 1::3, :]
                ve.tensor_scalar(sg[:], gates, 0.0, 2.0, ALU.is_ge, ALU.mult).then_inc(step, 1)
                ve.tensor_scalar(mg[:], gates, -1.0, None, ALU.mult).then_inc(step, 1)
                ve.tensor_scalar(gains, gains, 1.0, None, ALU.add).then_inc(step, 1)
                ve.wait_ge(step, 5 * k + 3)
                ve.scalar_tensor_tensor(out=mg[:], in0=mg[:], scalar=0.25, in1=gates, op0=ALU.max, op1=ALU.max).then_inc(step, 1)
                ve.wait_ge(step, 5 * k + 4)
                ve.scalar_tensor_tensor(out=gates, in0=sg[:], scalar=-1.0, in1=mg[:], op0=ALU.add, op1=ALU.mult).then_inc(step, 1)


def add_attention(nc, cfg, xT, hT, vall, gate, consts, dram):
    rel = cfg.rel
    name = "rel" if rel else "cau"
    with ExitStack() as ctx:
        sb = lambda n, s, d=F32: ctx.enter_context(nc.sbuf_tensor(f"{name}_{n}", s, d))
        sem = lambda n: nc.alloc_semaphore(f"{name}_{n}")
        ps = ctx.enter_context(nc.psum_tensor(f"{name}_ps", [P, 8, T], F32))
        S = lambda i: ps[:, i, :]
        BANK_A, BANK_B, BANK_T = ps[:, 4, :], ps[:, 5, :], lambda j: ps[:, 6 + j % 2, :]

        wqk = sb("wqk", [P, 2, P])
        wo = sb("wo", [P, P])
        vcur = sb("vcur", [P, NB, HG, QW])
        qs, ks = sb("qs", [P, T]), sb("ks", [P, T])
        q_hi, k_hi = sb("qhi", [P, T], F32R), sb("khi", [P, T], F32R)
        qz = [sb(f"qz{p}", [P, HG, T], F32R) for p in range(2)]
        kst = [sb(f"kst{p}", [P, T], F32R) for p in range(2)]
        probs = sb("probs", [P, 2, NB, T])
        negmax = sb("negmax", [P, HG, NB])
        pT = sb("pT", [P, HG, NB, T])
        o_sb, o_norm = sb("o", [P, T]), sb("onorm", [P, T])
        recip, spread = sb("recip", [P, NB * HG]), sb("spread", [P, NB * HG, QW])
        if rel:
            as_, a_hi, ast = sb("as", [P, T]), sb("ahi", [P, T], F32R), sb("ast", [P, T], F32R)
            wp_raw = sb("wpraw", [P, HG * 2 * P])
            wp_hi = sb("wphi", [P, HG * 2 * P], F32R)
            wp_all = sb("wpall", [P, NG, HG * 2 * P], F32R)
            wp = sb("wp", [P, HG, 2, P], F32R)
            rot1, rot2 = sb("rot1", [P, T]), sb("rot2", [P, T])
            gT = sb("gT", [P, 2, T + 1])
            diag = sb("diag", [P, NB, T])
            cols = sb("cols", [P, 5, NG])
            bqu, bqv, bks = sb("bqu", [P, NG]), sb("bqv", [P, NG]), sb("bks", [P, NG])
            gbo = sb("gbo", [P, B])

        wqk_loaded, wo_loaded, v_loaded = sem("wqk"), sem("wo"), sem("v")
        proj_ready, q_scaled, rounded, stacked = sem("proj"), sem("qsc"), sem("rnd"), sem("stk")
        scores_ready, max_ready, exp_ready = sem("sc"), sem("mx"), sem("exp")
        turned, copied_by_act, copied_by_dve = sem("tr"), sem("tra"), sem("trv")
        pv_ready, o_copied, sums_ready, recip_ready = sem("pv"), sem("oc"), sem("sum"), sem("rec")
        recip_spread, spread_ready, o_normed = sem("rsp"), sem("spr"), sem("on")
        wo_done, x_added = sem("wod"), sem("xa")
        if rel:
            wp_loaded, once, bias_step = sem("wp"), sem("once"), sem("bst")
            g_ready, rotated, g_summed, a_stacked = sem("g"), sem("rot"), sem("gs"), sem("ast")
            lu_ready, lower_masked, diag_masked = sem("lu"), sem("lm"), sem("dm")
            wp_split, wp_kept, wp_rounded = sem("wps"), sem("wpk"), sem("wpr")
        ve_passed, pool_passed = sem("vep"), sem("pop")
        NSTK = HG + 1
        NPROJ = 2 + rel
        BANK_O, BANK_R = (BANK_T(0), BANK_T(1)) if rel else (BANK_A, BANK_B)
        DVE_COPIES = () if rel else (1,)
        ACT_COPIES = tuple(j for j in range(NB) if j not in DVE_COPIES)
        NCA, NCV = len(ACT_COPIES), len(DVE_COPIES)

        with nc.Block() as setup:
            @setup.sync
            def _(sp):
                if rel:
                    sp.dma_start(cols[:], dram["cols"]).then_inc(once, 16)
                    for g in range(NG):
                        wait_past(sp, wp_split, g)
                        sp.dma_start(wp_raw[:], dram["wp"][g]).then_inc(wp_kept, 16)

            @setup.gpsimd
            def _(pool):
                for p in range(2):
                    pool.memset(qz[p][:].bitcast(F32), 0.0)
                if rel:
                    pool.memset(gT[:, :, T:T + 1], 0.0)
                    pool.memset(diag[:], 0.0)

            @setup.vector
            def _(ve):
                if not rel:
                    return
                ve.wait_ge(once, 16)
                ve.tensor_tensor(rot1[:, 0:NG], cols[:, 0, :], cols[:, 1, :], ALU.add).then_inc(bias_step, 1)
                ve.tensor_tensor(rot2[:, 0:NG], cols[:, 0, :], cols[:, 2, :], ALU.add).then_inc(bias_step, 1)
                ve.tensor_scalar(gbo[:], gate, cols[:, 4, 0:1], None, ALU.mult).then_inc(bias_step, 1)
                ve.tensor_copy(bks[:], cols[:, 3, :])
                ve.wait_ge(bias_step, 3)
                ve.tensor_scalar(bqu[:], rot1[:, 0:NG], cfg.scale, None, ALU.mult)
                ve.tensor_scalar(bqv[:], rot2[:, 0:NG], cfg.scale, None, ALU.mult)
                for b in range(B):
                    s = slice(b * T, (b + 1) * T)
                    ve.tensor_scalar(xT[:, s], xT[:, s], gbo[:, b:b + 1], None, ALU.add)
                for g in range(NG):
                    ve.wait_ge(wp_kept, 16 * (g + 1))
                    wait_past(ve, wp_split, g)
                    ve.tensor_copy(wp_hi[:], wp_raw[:]).then_inc(wp_rounded, 1)
                    ve.wait_ge(wp_rounded, g + 1)
                    ve.scalar_tensor_tensor(out=wp_all[:, g, :], in0=wp_hi[:].bitcast(F32), scalar=consts["neg_lo_k"],
                                            in1=wp_raw[:], op0=ALU.mult, op1=ALU.add).then_inc(wp_split, 1)

        block = ctx.enter_context(nc.Block())

        def loop(eng, body):
            def two(m):
                for p in range(2):
                    body(2 * m + p, p, isinstance(m, int) and 2 * m + p == NIT - 1)

            two(0)
            with eng.Fori(1, NIT // 2 - 1) as m:
                two(m)
            two(NIT // 2 - 1)

        def wait_copied(eng, head, j):
            if j in DVE_COPIES:
                wait_past(eng, copied_by_dve, NCV * head + DVE_COPIES.index(j) + 1)
            else:
                wait_past(eng, copied_by_act, NCA * head + ACT_COPIES.index(j) + 1)

        @block.sync
        def _(sp):
            def load_wqk(n):
                wait_past(sp, proj_ready, 2 * n)
                sp.dma_start(wqk[:], dram["wqk"][bass.ds(n % NG, 1)].rearrange("o p (k m) -> p (o k) m", k=2)).then_inc(wqk_loaded, 16)

            def load_wp(n):
                wait_past(sp, g_ready, HG * n)
                sp.dma_start(wp[:].bitcast(F32), wp_all[:, bass.ds(n % NG, 1), :].bitcast(F32).rearrange(
                    "p o (h k m) -> p (o h) k m", h=HG, k=2)).then_inc(wp_loaded, 16)

            def body(n, p, last):
                if not last:
                    load_wqk(n + 1)
                wait_past(sp, pv_ready, n)
                sp.dma_start(vcur[:], vall[:, bass.ds((n // NG) * NB, NB), bass.ds((n % NG) * HG, HG), :]).then_inc(v_loaded, 16)
                wait_past(sp, wo_done, n)
                sp.dma_start(wo[:], dram["wo"][bass.ds(n % NG, 1)].rearrange("o p m -> p (o m)")).then_inc(wo_loaded, 16)
                if rel and not last:
                    load_wp(n + 1)

            load_wqk(0)
            if rel:
                load_wp(0)
            loop(sp, body)

        @block.tensor
        def _(pe):
            def project(n):
                pe.wait_ge(wqk_loaded, 16 * (n + 1))
                wait_past(pe, q_scaled, NPROJ * n)
                if rel and not (isinstance(n, int) and n == 0):
                    pe.wait_ge(rotated, 2 * (HG * (n - 1) + 3))
                elif not rel:
                    wait_past(pe, x_added, n - 2)
                batch = hT[:, bass.ds((n // NG) * T, T)]
                pe.matmul(BANK_A, wqk[:, 0, :], batch, start=True, stop=True).then_inc(proj_ready, 1)
                pe.matmul(BANK_B, wqk[:, 1, :], batch, start=True, stop=True).then_inc(proj_ready, 1)

            def frequencies(n, h):
                if h == 0:
                    pe.wait_ge(wp_loaded, 16 * (n + 1))
                    pe.wait_ge(a_stacked, n + 1)
                    pe.wait_ge(q_scaled, NPROJ * (n + 1))
                wait_past(pe, diag_masked, HG * NB * n + NB * h)
                pe.matmul(BANK_A, wp[:, h, 0, :], ast[:], start=True, stop=True)
                pe.matmul(BANK_B, wp[:, h, 1, :], ast[:], start=True, stop=True).then_inc(g_ready, 1)

            def diagonal(n, h, i, last=False):
                if i == 0:
                    pe.wait_ge(g_summed, HG * n + h + 1)
                    if h == 2 and not last:
                        pe.wait_ge(q_scaled, NPROJ * (n + 2))
                if i >= 2:
                    pe.wait_ge(diag_masked, HG * NB * n + NB * h + i - 1)
                d, w = i * P, min(DIAG, T - i * P)
                bank, g = ps[:, 4 + i % 2, :], gT[:, h % 2, :]
                pe.matmul(bank[:, 0:w], g[:, d:d + P], consts["pe"][:, T + d:T + d + w], start=True, stop=True,
                          skip_group_check=True)
                pe.matmul(bank[:, DIAG:DIAG + w], g[:, d + 1:d + P + 1], consts["pe"][:, d:d + w], start=True, stop=True,
                          skip_group_check=True).then_inc(lu_ready, 1)

            def scores(n, p, h, i):
                base = HG * NB * n + NB * h
                if h == 0 and i == 0:
                    pe.wait_ge(stacked, NSTK * (n + 1))
                wait_past(pe, exp_ready, base + i + 1 - NB)
                d, e = i * P, (i + 1) * P
                q, k = qz[p][:, h, d:e], kst[p]
                if not rel:
                    w = max(e, 2 * P)
                    pe.matmul(S(i)[:, 0:w], q, k[:, 0:w], start=True, stop=False, skip_group_check=True)
                    pe.matmul(S(i)[:, d:e], consts["ident_bf"], consts["causal"], start=False, stop=True,
                              skip_group_check=True).then_inc(scores_ready, 1)
                    return
                g = gT[:, h % 2, :]
                mm = pe.matmul(S(i), q, k[:], start=True, stop=False, skip_group_check=True)
                if i > 0:
                    mm = pe.matmul(S(i)[:, 0:d], g[:, d:e], consts["pe"][:, T:T + d], start=False, stop=False, skip_group_check=True)
                if i < NB - 1:
                    mm = pe.matmul(S(i)[:, e + 1:T], g[:, d + 1:e + 1], consts["pe"][:, e + 1:T], start=False, stop=False,
                                   skip_group_check=True)
                mm.then_inc(scores_ready, 1)

            def transposes(n, h, j):
                base = HG * NB * n + NB * h
                pe.wait_ge(exp_ready, base + NB)
                wait_copied(pe, HG * n + h - (j < 2), (j - 2) % NB)
                if rel and h == 0 and j == 0:
                    wait_past(pe, x_added, n)
                for i in range(0 if rel else j, NB):
                    tr = pe.transpose(BANK_T(j)[:, i * P:(i + 1) * P], probs[:, h % 2, i, j * P:(j + 1) * P], consts["ident"])
                tr.then_inc(turned, 1)

            def values(n, last=False):
                wait_copied(pe, HG * n + HG - 1, ACT_COPIES[-1])
                if DVE_COPIES:
                    wait_copied(pe, HG * n + HG - 1, DVE_COPIES[-1])
                if not rel and not last:
                    pe.wait_ge(q_scaled, NPROJ * (n + 3))
                pe.wait_ge(v_loaded, 16 * (n + 1))
                for j in range(NB):
                    i0 = 0 if rel else j * P
                    for h in range(HG):
                        mm = pe.matmul(BANK_O[h * QW:(h + 1) * QW, i0:T], vcur[:, j, h, :], pT[:, h, j, i0:T],
                                       start=(j == 0), stop=(j == NB - 1), skip_group_check=True)
                mm.then_inc(pv_ready, 1)

            def sums(n):
                pe.wait_ge(o_copied, n + 1)
                for i in range(NB):
                    mm = pe.matmul(BANK_R[:, i * HG:(i + 1) * HG], o_sb[:, i * P:(i + 1) * P], consts["pick"],
                                   start=True, stop=True, skip_group_check=True)
                mm.then_inc(sums_ready, 1)

            def spread_recips(n):
                pe.wait_ge(recip_spread, n + 1)
                for i in range(NB):
                    mm = pe.matmul(BANK_R[:, i * P:(i + 1) * P], spread[:, i * HG:(i + 1) * HG, :].rearrange("p h q -> p (h q)"),
                                   consts["ident"], start=True, stop=True, skip_group_check=True)
                mm.then_inc(spread_ready, 1)

            def project_out(n):
                pe.wait_ge(o_normed, n + 1)
                pe.wait_ge(wo_loaded, 16 * (n + 1))
                pe.matmul(BANK_O, wo[:], o_norm[:], start=True, stop=True).then_inc(wo_done, 1)

            def body(n, p, last):
                first = isinstance(n, int) and n == 0
                for h in range(HG):
                    before = (n - 1, HG - 1) if h == 0 else (n, h - 1)
                    after = (n + 1, 0) if h == HG - 1 else (n, h + 1)
                    turn = h > 0 or not first
                    tail = not first and h == 1
                    if rel:
                        diagonal(n, h, 0, last)
                        diagonal(n, h, 1)
                        scores(n, p, h, 0)
                        if tail:
                            sums(n - 1)
                        diagonal(n, h, 2)
                        diagonal(n, h, 3)
                        scores(n, p, h, 1)
                        if tail:
                            spread_recips(n - 1)
                        elif turn and h != 1:
                            transposes(*before, 0)
                        if not (h == HG - 1 and last):
                            frequencies(*after)
                        scores(n, p, h, 2)
                        if tail:
                            project_out(n - 1)
                        elif turn and h != 1:
                            transposes(*before, 1)
                        if h == 1 and not last:
                            project(n + 1)
                        scores(n, p, h, 3)
                        for j in range(0 if h == 1 else 2, NB):
                            if turn:
                                transposes(*before, j)
                    else:
                        scores(n, p, h, 0)
                        scores(n, p, h, 1)
                        if h == 0 and not last:
                            project(n + 1)
                        scores(n, p, h, 2)
                        scores(n, p, h, 3)
                        if tail:
                            sums(n - 1)
                        if h == 2 and not first:
                            project_out(n - 1)
                        for j in range(NB):
                            if turn:
                                transposes(*before, j)
                        if tail:
                            spread_recips(n - 1)
                    if h == 0 and not first:
                        values(n - 1, last)

            project(0)
            if rel:
                frequencies(0, 0)
            loop(pe, body)
            for j in range(NB):
                transposes(NIT - 1, HG - 1, j)
            values(NIT - 1, True)
            sums(NIT - 1)
            spread_recips(NIT - 1)
            project_out(NIT - 1)

        @block.scalar
        def _(act):
            def read(dst, bank, bias, scale):
                if bias is None:
                    ins = act.activation(dst[:], bank, ACT.Copy, scale=scale)
                else:
                    ins = act.activation(dst[:], bank, ACT.Identity, bias=bias, scale=scale)
                ins.then_inc(q_scaled, 1)

            def read_projections(n):
                g = n % NG
                act.wait_ge(proj_ready, 2 * n + 1)
                wait_past(act, stacked, NSTK * n)
                if rel:
                    read(as_, BANK_A, bqv[:, bass.ds(g, 1)], cfg.scale)
                read(qs, BANK_A, bqu[:, bass.ds(g, 1)] if rel else None, cfg.scale)
                act.wait_ge(proj_ready, 2 * n + 2)
                read(ks, BANK_B, bks[:, bass.ds(g, 1)] if rel else None, 1.0)

            def exp(n, h, i):
                base = HG * NB * n + NB * h
                if i == 0:
                    wait_past(act, turned, base - NB)
                w = T if rel else (i + 1) * P
                act.wait_ge(max_ready, base + i + 1)
                act.activation(probs[:, h % 2, i, 0:w], S(i)[:, 0:w], ACT.Exp, bias=negmax[:, h, i:i + 1],
                               scale=-1.0 if rel else 1.0).then_inc(exp_ready, 1)

            def copy(n, h, j):
                if h == 0 and j == ACT_COPIES[0]:
                    wait_past(act, pv_ready, n)
                i0 = 0 if rel else j * P
                act.wait_ge(turned, HG * NB * n + NB * h + j + 1)
                act.copy(pT[:, h, j, i0:T], BANK_T(j)[:, i0:T]).then_inc(copied_by_act, 1)

            def copy_values(n):
                act.wait_ge(pv_ready, n + 1)
                wait_past(act, o_normed, n)
                act.copy(o_sb[:], BANK_O).then_inc(o_copied, 1)

            def body(n, p, last):
                first = isinstance(n, int) and n == 0
                for h in range(HG):
                    before = (n - 1, HG - 1) if h == 0 else (n, h - 1)
                    turn = h > 0 or not first
                    if h == 1 and not first:
                        copy_values(n - 1)
                    after_exp = {1: (0,), 2: (1,), 3: (2, 3)}
                    if rel and h == 1:
                        after_exp = {3: (0, 1, 2, 3)}
                    for i in range(NB):
                        if i == (3 if rel else 2) and h == (1 if rel else 0) and not last:
                            read_projections(n + 1)
                        exp(n, h, i)
                        for j in after_exp.get(i, ()):
                            if turn and j in ACT_COPIES:
                                copy(*before, j)

            read_projections(0)
            loop(act, body)
            for j in ACT_COPIES:
                copy(NIT - 1, HG - 1, j)
            copy_values(NIT - 1)

        @block.vector
        def _(ve):
            def stack_query(n, p, h):
                r = slice(h * QW, (h + 1) * QW)
                ve.wait_ge(rounded, NPROJ * n + NPROJ - 1)
                wait_past(ve, scores_ready, HG * NB * (n - 1))
                ve.scalar_tensor_tensor(out=qz[p][r, h, :], in0=q_hi[r, :].bitcast(F32), scalar=consts["neg_lo_q"][r, :],
                                        in1=qs[r, :], op0=ALU.mult, op1=ALU.add).then_inc(stacked, 1)

            def stack_keys(n, p):
                ve.wait_ge(rounded, NPROJ * (n + 1))
                wait_past(ve, scores_ready, HG * NB * (n - 1))
                ve.scalar_tensor_tensor(out=kst[p][:], in0=k_hi[:].bitcast(F32), scalar=consts["neg_lo_k"],
                                        in1=ks[:], op0=ALU.mult, op1=ALU.add).then_inc(stacked, 1)

            def stack_positions(n):
                ve.wait_ge(rounded, NPROJ * n + 1)
                wait_past(ve, g_ready, HG * n)
                ve.scalar_tensor_tensor(out=ast[:], in0=a_hi[:].bitcast(F32), scalar=consts["neg_lo_q"],
                                        in1=as_[:], op0=ALU.mult, op1=ALU.add).then_inc(a_stacked, 1)

            def copy(n, h, j):
                wait_past(ve, pv_ready, n)
                i0 = 0 if rel else j * P
                ve.wait_ge(turned, HG * NB * n + NB * h + j + 1)
                ve.tensor_copy(pT[:, h, j, i0:T], BANK_T(j)[:, i0:T]).then_inc(copied_by_dve, 1)

            def rotate(n, h):
                ve.wait_ge(g_ready, HG * n + h + 1)
                wait_past(ve, g_summed, HG * n + h)
                ve.tensor_tensor(rot1[:], BANK_A, consts["cos"], ALU.mult).then_inc(rotated, 1)
                ve.tensor_tensor(rot2[:], BANK_B, consts["sin"], ALU.mult).then_inc(rotated, 1)

            def mask(n, h, i):
                base = HG * NB * n + NB * h
                w = min(DIAG, T - i * P)
                d, bank = slice(i * P, i * P + w), ps[:, 4 + i % 2, :]
                ve.wait_ge(lu_ready, base + i + 1)
                wait_past(ve, max_ready, base + i + 1 - NB)
                ve.tensor_tensor(diag[:, i, d], bank[:, 0:w], consts["lower"][:, 0:w], ALU.mult).then_inc(lower_masked, 1)
                ve.wait_ge(lower_masked, base + i + 1)
                ve.sem_inc(ve_passed, 1)
                ve.copy_predicated(diag[:, i, d], consts["upper"][:, 0:w], bank[:, DIAG:DIAG + w]).then_inc(diag_masked, 1)

            def maximum(n, h, i):
                base = HG * NB * n + NB * h
                ve.wait_ge(scores_ready, base + i + 1)
                if i == 0:
                    wait_past(ve, exp_ready, base + NB - HG * NB)
                if rel:
                    ve.wait_ge(diag_masked, base + i + 1)
                    ve.sem_inc(ve_passed, 1)
                    ve.tensor_tensor_reduce(S(i), S(i), diag[:, i, :], -1.0, -NEG, ALU.add, ALU.min,
                                            negmax[:, h, i:i + 1]).then_inc(max_ready, 1)
                else:
                    ve.tensor_reduce(negmax[:, h, i:i + 1], S(i)[:, 0:(i + 1) * P], AX_X, ALU.max, negate=True).then_inc(max_ready, 1)

            def reciprocals(n):
                ve.wait_ge(sums_ready, n + 1)
                ve.reciprocal(recip[:], BANK_R[:, 0:NB * HG]).then_inc(recip_ready, 1)
                ve.wait_ge(recip_ready, n + 1)
                wait_past(ve, spread_ready, n)
                ve.tensor_copy(spread[:], recip[:].unsqueeze(2).broadcast_to([P, NB * HG, QW])).then_inc(recip_spread, 1)

            def normalise(n):
                ve.wait_ge(spread_ready, n + 1)
                wait_past(ve, wo_done, n)
                ve.tensor_tensor(o_norm[:], o_sb[:], BANK_R, ALU.mult).then_inc(o_normed, 1)

            def add_to_x(n):
                ve.wait_ge(wo_done, n + 1)
                wait_past(ve, x_added, n)
                s = bass.ds((n // NG) * T, T)
                ve.scalar_tensor_tensor(out=xT[:, s], in0=BANK_O, scalar=gate[:, bass.ds(n // NG, 1)],
                                        in1=xT[:, s], op0=ALU.mult, op1=ALU.add).then_inc(x_added, 1)

            def body(n, p, last):
                first = isinstance(n, int) and n == 0
                for h in range(HG):
                    before = (n - 1, HG - 1) if h == 0 else (n, h - 1)
                    after = (n + 1, 0) if h == HG - 1 else (n, h + 1)
                    tail = not first and h == 1
                    stack = not last
                    if rel:
                        mask(n, h, 0)
                        mask(n, h, 1)
                        maximum(n, h, 0)
                        mask(n, h, 2)
                        mask(n, h, 3)
                        if tail:
                            reciprocals(n - 1)
                        maximum(n, h, 1)
                        if not (h == HG - 1 and last):
                            rotate(*after)
                        if tail:
                            normalise(n - 1)
                        if stack and h == 3:
                            stack_query(n + 1, 1 - p, 1)
                        maximum(n, h, 2)
                        if tail:
                            add_to_x(n - 1)
                        if stack and h == 3:
                            stack_query(n + 1, 1 - p, 2)
                        maximum(n, h, 3)
                        if stack and h == 2:
                            stack_positions(n + 1)
                            stack_query(n + 1, 1 - p, 0)
                        if stack and h == 3:
                            stack_query(n + 1, 1 - p, 3)
                            stack_keys(n + 1, 1 - p)
                    else:
                        maximum(n, h, 0)
                        maximum(n, h, 1)
                        if h == 2 and not first:
                            normalise(n - 1)
                        maximum(n, h, 2)
                        maximum(n, h, 3)
                        if tail:
                            reciprocals(n - 1)
                        if h > 0 or not first:
                            copy(*before, 1)
                        if h == 2 and not first:
                            add_to_x(n - 1)
                        if stack and h in (1, 2):
                            stack_query(n + 1, 1 - p, 2 * h - 2)
                            stack_query(n + 1, 1 - p, 2 * h - 1)
                        if stack and h == 3:
                            stack_keys(n + 1, 1 - p)

            if rel:
                stack_positions(0)
            for h in range(HG):
                stack_query(0, 0, h)
            stack_keys(0, 0)
            if rel:
                rotate(0, 0)
            loop(ve, body)
            for j in DVE_COPIES:
                copy(NIT - 1, HG - 1, j)
            reciprocals(NIT - 1)
            normalise(NIT - 1)
            add_to_x(NIT - 1)

        @block.gpsimd
        def _(pool):
            def high(n, k, dst, src):
                pool.wait_ge(q_scaled, NPROJ * n + k + 1)
                wait_past(pool, stacked, NSTK * n)
                pool.sem_inc(pool_passed, 1)
                pool.tensor_copy(dst[:], src[:]).then_inc(rounded, 1)

            def high_queries(n):
                if rel:
                    high(n, 0, a_hi, as_)
                high(n, NPROJ - 2, q_hi, qs)

            def high_keys(n):
                high(n, NPROJ - 1, k_hi, ks)

            def sum_rotated(n, h):
                pool.wait_ge(rotated, 2 * (HG * n + h + 1))
                wait_past(pool, scores_ready, HG * NB * n + NB * (h - 1))
                pool.tensor_tensor(gT[:, h % 2, 0:T], rot1[:], rot2[:], ALU.add).then_inc(g_summed, 1)

            def body(n, p, last):
                for h in range(HG):
                    if rel and not (h == HG - 1 and last):
                        sum_rotated(*((n + 1, 0) if h == HG - 1 else (n, h + 1)))
                    if h == (1 if rel else 0) and not last:
                        high_queries(n + 1)
                    if h == (2 if rel else 0) and not last:
                        high_keys(n + 1)

            high_queries(0)
            high_keys(0)
            if rel:
                sum_rotated(0, 0)
            loop(pool, body)


def add_router(nc, cfg, hT, CT, consts, dram):
    E, NT, name = cfg.E, NTOK // P, "r1" if cfg.rel else "r0"
    G, GE = 8, 8
    BIG = 3e38
    with ExitStack() as ctx:
        sb = lambda n, s, d=F32: ctx.enter_context(nc.sbuf_tensor(f"{name}_{n}", s, d))
        sem = lambda n: nc.alloc_semaphore(f"{name}_{n}")
        lg_ps = ctx.enter_context(nc.psum_tensor(f"{name}_lg", [P, NT, 64], F32))
        tp_ps = ctx.enter_context(nc.psum_tensor(f"{name}_tp", [P, B, T], F32))
        gw, bias = sb("gw", [P, E]), sb("bias", [P, E])
        score, biased, rep = sb("score", [P, NT, E]), sb("biased", [P, NT, E]), sb("rep", [P, NT, E])
        v8, red, rcp = sb("v8", [P, NT, 8]), sb("red", [P, NT]), sb("rcp", [P, NT])
        sel, comb = sb("sel", [P, NT, E]), sb("comb", [P, NT, E])
        stack = sb("stack", [P, NT, P], F32R)
        if cfg.rel:
            masked = sb("masked", [P, NT, E])
            gmask = sb("gmask", [P, NT, G], U32)
            emask = sb("emask", [P, NT * G, GE], U32)
            hi1, lo1, t1, t2 = (sb(n, [P, NT * G, 4]) for n in ("hi1", "lo1", "t1", "t2"))
            gs, grep = sb("gs", [P, NT, G]), sb("grep", [P, NT, G])
        loaded, logits_ready, act_ready, step = sem("ld"), sem("lg"), sem("act"), sem("st")
        stacked, turned, in_ready = sem("stk"), sem("tr"), sem("in")
        block = ctx.enter_context(nc.Block())
        logits = lg_ps[:, :, 0:E]

        def over_experts(a):
            return a.unsqueeze(2).broadcast_to([P, NT, E])

        @block.sync
        def _(sp):
            sp.dma_start(gw[:], dram["gate"]).then_inc(loaded, 16)
            sp.dma_start(bias[:], dram["bias"]).then_inc(loaded, 16)

        @block.gpsimd
        def _(pool):
            pool.memset(stack[:].bitcast(F32), 0.0).then_inc(in_ready, 1)
            if cfg.rel:
                pool.memset(masked[:], 0.0).then_inc(in_ready, 1)

        @block.tensor
        def _(pe):
            pe.wait_ge(loaded, 32)
            for t in range(NT):
                mm = pe.matmul(lg_ps[:, t, 0:E], hT[:, t * P:(t + 1) * P], gw[:], start=True, stop=True)
            mm.then_inc(logits_ready, 1)
            pe.wait_ge(stacked, 2)
            for t in range(NT):
                tr = pe.transpose(tp_ps[:, t // NB, (t % NB) * P:(t % NB + 1) * P], stack[:, t, :].bitcast(F32), consts["ident"])
                if t % NB == NB - 1:
                    tr.then_inc(turned, 1)

        @block.scalar
        def _(act):
            if cfg.rel:
                act.wait_ge(logits_ready, 1)
                act.activation(score[:], logits, ACT.Sigmoid).then_inc(act_ready, 1)
            else:
                act.wait_ge(step, 2)
                act.activation(rep[:], biased[:], ACT.Exp).then_inc(act_ready, 1)
            for b in range(B):
                act.wait_ge(turned, b + 1)
                act.copy(CT[:, b * T:(b + 1) * T], tp_ps[:, b, :])

        @block.vector
        def _(ve):
            done = [0]

            def chain(ins):
                done[0] += 1
                ins.then_inc(step, 1)
                ve.wait_ge(step, done[0])

            ve.wait_ge(loaded, 32)
            ve.wait_ge(in_ready, 1 + cfg.rel)
            if not cfg.rel:
                ve.wait_ge(logits_ready, 1)
                chain(ve.tensor_reduce(red[:], logits, AX_X, ALU.max))
                chain(ve.tensor_tensor(biased[:], logits, over_experts(red[:]), ALU.subtract))
                ve.wait_ge(act_ready, 1)
                chain(ve.reduce_sum(red[:], rep[:], AX_X))
                chain(ve.reciprocal(rcp[:], red[:]))
                chain(ve.tensor_tensor(score[:], rep[:], over_experts(rcp[:]), ALU.mult))
            else:
                ve.wait_ge(act_ready, 1)
            bias_all = bias[:].unsqueeze(1).broadcast_to([P, NT, E])
            chain(ve.tensor_tensor(biased[:], score[:], bias_all, ALU.add))

            def pick_top(out, values, k):
                for t in range(NT):
                    ins = ve.max(v8[:, t, :], values[:, t, :])
                chain(ins)
                if k < 8:
                    chain(ve.memset(v8[:, :, k:8], BIG))
                for t in range(NT):
                    ins = ve.match_replace(out[:, t, :], v8[:, t, :], values[:, t, :], -BIG)
                chain(ins)

            if not cfg.rel:
                pick_top(rep[:], biased[:], 2)
                chain(ve.tensor_scalar(sel[:], rep[:], -1e38, None, ALU.is_le))
                chain(ve.tensor_tensor(comb[:], score[:], sel[:], ALU.mult))
            else:
                def pairs(a, n):
                    v = a.rearrange("p g (n two) -> p g n two", two=2)
                    return v[:, :, :, 0], v[:, :, :, 1]

                v = biased[:].rearrange("p t (g e) -> p (t g) e", e=GE)
                a, b_ = pairs(v, 4)
                chain(ve.tensor_tensor(hi1[:], a, b_, ALU.max))
                chain(ve.tensor_tensor(lo1[:], a, b_, ALU.min))
                w = 4
                while w > 1:
                    ha, hb = pairs(hi1[:, :, 0:w], w // 2)
                    la, lb = pairs(lo1[:, :, 0:w], w // 2)
                    u = w // 2
                    chain(ve.tensor_tensor(t1[:, :, 0:u], ha, hb, ALU.min))
                    chain(ve.tensor_tensor(t2[:, :, 0:u], la, lb, ALU.max))
                    chain(ve.tensor_tensor(t2[:, :, 0:u], t1[:, :, 0:u], t2[:, :, 0:u], ALU.max))
                    chain(ve.tensor_tensor(t1[:, :, 0:u], ha, hb, ALU.max))
                    chain(ve.tensor_copy(hi1[:, :, 0:u], t1[:, :, 0:u]))
                    chain(ve.tensor_copy(lo1[:, :, 0:u], t2[:, :, 0:u]))
                    w = u
                chain(ve.tensor_tensor(gs[:].rearrange("p t g -> p (t g)"), hi1[:, :, 0], lo1[:, :, 0], ALU.add))
                pick_top(grep[:], gs[:], 4)
                chain(ve.tensor_scalar(gmask[:], grep[:], -1e38, None, ALU.is_le))
                chain(ve.tensor_copy(emask[:], gmask[:].rearrange("p t g -> p (t g)").unsqueeze(2).broadcast_to([P, NT * G, GE])))
                chain(ve.copy_predicated(masked[:].rearrange("p t (g e) -> p (t g) e", e=GE), emask[:], v))
                pick_top(rep[:], masked[:], 8)
                chain(ve.tensor_scalar(sel[:], rep[:], -1e38, None, ALU.is_le))
                chain(ve.tensor_tensor(sel[:], score[:], sel[:], ALU.mult))
                chain(ve.reduce_sum(red[:], sel[:], AX_X))
                chain(ve.tensor_scalar(red[:], red[:], 1e-20, None, ALU.add))
                chain(ve.reciprocal(rcp[:], red[:]))
                chain(ve.tensor_scalar(rcp[:], rcp[:], 2.5, None, ALU.mult))
                chain(ve.tensor_tensor(comb[:], sel[:], over_experts(rcp[:]), ALU.mult))
            ve.tensor_copy(stack[:, :, 0:E], comb[:]).then_inc(stacked, 1)
            ve.wait_ge(stacked, 1)
            ve.tensor_tensor(stack[:, :, 64:64 + E], comb[:], stack[:, :, 0:E].bitcast(F32), ALU.subtract).then_inc(stacked, 1)


def add_moe(nc, cfg, xT, h_hi, h_lo, CT, gate, dram):
    up, name = cfg.up, "m1" if cfg.rel else "m0"
    U = cfg.units + 2
    STEPS = U // 2
    SEL, DOWN = up, up + 1
    NSH = 2 * B
    with ExitStack() as ctx:
        sb = lambda n, s, d=F32: ctx.enter_context(nc.sbuf_tensor(f"{name}_{n}", s, d))
        sem = lambda n: nc.alloc_semaphore(f"{name}_{n}")
        ps = ctx.enter_context(nc.psum_tensor(f"{name}_ps", [P, 8, T], F32))
        w = [sb(f"w{q}", [P, up + 2, P]) for q in range(2)]
        w_hi = [sb(f"whi{q}", [P, up + 1, P], F32R) for q in range(2)]
        w_lo = [sb(f"wlo{q}", [P, up, P], F32R) for q in range(2)]
        acts = sb("acts", [P, 2, T])
        scaled = sb("scaled", [P, 2, T])
        hidden = sb("hidden", [P, 2, T])
        w_loaded = [sem("wl0"), sem("wl1")]
        w_rounded, w_split = sem("wr"), sem("ws")
        up_ready, comb_ready, act_ready = sem("up"), sem("cb"), sem("act")
        scaled_ready, hidden_ready, down_done, added = sem("sc"), sem("hid"), sem("dn"), sem("add")
        A = lambda m: ps[:, 4 + m % 2, :]
        Bk = ps[:, 6, :]
        C = lambda m: ps[:, 6 + m % 2, :] if up == 1 else ps[:, 7, :]
        block = ctx.enter_context(nc.Block())

        def steps(eng, body):
            body(0, False)
            with eng.Fori(1, STEPS - 1) as k:
                body(k, False)
            body(STEPS - 1, True)

        @block.sync
        def _(sp):
            def body(k, last):
                for q in range(2):
                    u = 2 * k + q
                    wait_past(sp, w_loaded[q], 16 * k)
                    wait_past(sp, down_done, B * u - B)
                    sp.dma_start(w[q][:], dram["units"][bass.ds(u, 1)].rearrange("o p (k m) -> p (o k) m", k=up + 2)).then_inc(w_loaded[q], 16)

            steps(sp, body)

        @block.tensor
        def _(pe):
            def down(m, q, b, first):
                pe.wait_ge(hidden_ready, m + 1)
                pe.matmul(ps[:, b, :], w[q][:, DOWN, :], hidden[:, b % 2, :], start=first, stop=False,
                          skip_group_check=True).then_inc(down_done, 1)

            def body(k, last):
                shared = isinstance(k, int) and k == 0
                for q in range(2):
                    u = 2 * k + q
                    pe.wait_ge(w_split, u + 1)
                    for b in range(B):
                        m = B * u + b
                        tok = slice(b * T, (b + 1) * T)
                        for a in range(up):
                            bank = A(b) if a == 0 else Bk
                            if a == 0:
                                wait_past(pe, act_ready, m - 1)
                            else:
                                wait_past(pe, hidden_ready, m)
                            pe.matmul(bank, w_hi[q][:, a, :], h_hi[:, tok], start=True, stop=False)
                            pe.matmul(bank, w_hi[q][:, a, :], h_lo[:, tok], start=False, stop=False)
                            mm = pe.matmul(bank, w_lo[q][:, a, :], h_hi[:, tok], start=False, stop=True)
                        mm.then_inc(up_ready, 1)
                        if not shared:
                            pe.wait_ge(hidden_ready, m - 1 if up == 1 else m)
                            pe.matmul(C(b), w_hi[q][:, SEL, :], CT[:, tok], start=True, stop=True).then_inc(comb_ready, 1)
                        if shared and m == 0:
                            continue
                        pb, pq = (b - 1, q) if b else (B - 1, 1 - q)
                        down(m - 1, pq, pb, first=shared and m - 1 < B)
                if last:
                    down(B * U - 1, 1, B - 1, False)

            steps(pe, body)

        @block.scalar
        def _(act):
            def body(k, last):
                for q in range(2):
                    for b in range(B):
                        m = B * (2 * k + q) + b
                        act.wait_ge(up_ready, m + 1)
                        wait_past(act, hidden_ready, m - 1)
                        act.activation(acts[:, b % 2, :], A(b), ACT.Relu if up == 1 else ACT.Silu).then_inc(act_ready, 1)

            steps(act, body)

        def split(ve, u, k, q):
            ve.wait_ge(w_loaded[q], 16 * (k + 1))
            wait_past(ve, up_ready, B * (u - 1))
            wait_past(ve, hidden_ready, B * (u - 1))
            ve.tensor_copy(w_hi[q][:], w[q][:, 0:up + 1, :]).then_inc(w_rounded, 1)
            ve.wait_ge(w_rounded, u + 1)
            ve.tensor_tensor(w_lo[q][:], w[q][:, 0:up, :], w_hi[q][:, 0:up, :].bitcast(F32), ALU.subtract).then_inc(w_split, 1)

        @block.vector
        def _(ve):
            split(ve, 0, 0, 0)

            def body(k, last):
                shared = isinstance(k, int) and k == 0
                for q in range(2):
                    u = 2 * k + q
                    for b in range(B):
                        m = B * u + b
                        if b == 3 and not (last and q == 1):
                            split(ve, u + 1, k + q, 1 - q)
                        if up == 2:
                            ve.wait_ge(act_ready, m + 1)
                            wait_past(ve, down_done, m - 1)
                            if shared:
                                ve.tensor_tensor(hidden[:, b % 2, :], Bk, acts[:, b % 2, :], ALU.mult).then_inc(hidden_ready, 1)
                                continue
                            ve.tensor_tensor(scaled[:, b % 2, :], Bk, acts[:, b % 2, :], ALU.mult).then_inc(scaled_ready, 1)
                            ve.wait_ge(comb_ready, m + 1 - NSH)
                            ve.wait_ge(scaled_ready, m + 1 - NSH)
                            ve.tensor_tensor(hidden[:, b % 2, :], C(b), scaled[:, b % 2, :], ALU.mult).then_inc(hidden_ready, 1)
                        elif not shared:
                            ve.wait_ge(act_ready, m + 1)
                            ve.wait_ge(comb_ready, m + 1 - NSH)
                            ve.wait_ge(hidden_ready, m - 1)
                            ve.tensor_tensor(scaled[:, b % 2, :], C(b), acts[:, b % 2, :], ALU.mult).then_inc(scaled_ready, 1)

            steps(ve, body)
            for b in range(B):
                ve.wait_ge(down_done, B * (U - 1) + b + 1)
                s = slice(b * T, (b + 1) * T)
                ve.scalar_tensor_tensor(out=xT[:, s], in0=ps[:, b, :], scalar=gate[:, b:b + 1], in1=xT[:, s],
                                        op0=ALU.mult, op1=ALU.add).then_inc(added, 1)

        @block.gpsimd
        def _(pool):
            if up == 2:
                return

            def body(k, last):
                shared = isinstance(k, int) and k == 0
                for q in range(2):
                    for b in range(B):
                        m = B * (2 * k + q) + b
                        wait_past(pool, down_done, m - 1)
                        pool.wait_ge(act_ready, m + 1)
                        other = acts if shared else scaled
                        if not shared:
                            pool.wait_ge(scaled_ready, m + 1 - NSH)
                        pool.tensor_tensor(hidden[:, b % 2, :], acts[:, b % 2, :], other[:, b % 2, :], ALU.mult).then_inc(hidden_ready, 1)

            steps(pool, body)


N_CONST = 2 * P + HG + 2 * DIAG + 4 * T + 2


def build_program(nc, a, out, upto=99):
    with ExitStack() as ctx:
        sb = lambda n, s, d=F32: ctx.enter_context(nc.sbuf_tensor(n, s, d))
        xT, hT = sb("xT", [P, NTOK]), sb("hT", [P, NTOK])
        const = sb("const", [P, N_CONST])
        bf = sb("const_bf", [P, 2, P], BF16)
        mods = [sb(f"mod{k}", [P, 6, B]) for k in range(2)]
        mean_w, eps_col = sb("mean_w", [P, P]), sb("eps", [P, 1])
        wv, gb, bv = [sb(f"wv{k}", [P, D]) for k in range(2)], sb("ln_gb", [P, 2]), sb("bv", [P, D])
        load_done, out_done = (nc.alloc_semaphore(n) for n in ("load_done", "out_done"))

        consts, at = {}, 0
        for key, n in (("ident", P), ("causal_f", P), ("pick", HG), ("lower", DIAG), ("upper_f", DIAG), ("pe", 2 * T), ("cos", T), ("sin", T),
                       ("neg_lo_q", 1), ("neg_lo_k", 1)):
            consts[key] = const[:, at:at + n]
            at += n
        upper = sb("upper", [P, DIAG], U32)
        consts["upper"] = upper[:]
        consts["ident_bf"], consts["causal"] = bf[:, 0, :], bf[:, 1, :]

        with nc.Block() as block:
            @block.sync
            def _(sp):
                for dst, src in ((xT[:], a["xT"]), (const[:, 0:at], a["const"]), (wv[0][:], a["wv0"]), (wv[1][:], a["wv1"]),
                                 (gb[:], a["ln_gb"]), (bv[:], a["bv"])):
                    sp.dma_start(dst, src).then_inc(load_done, 16)
                sp.wait_ge(load_done, 96)

            @block.vector
            def _(ve):
                ve.memset(mean_w[:], 1.0 / D)
                ve.memset(eps_col[:], LN_EPS)
                ve.wait_ge(load_done, 96)
                ve.tensor_copy(bf[:, 0, :], consts["ident"])
                ve.tensor_copy(bf[:, 1, :], consts["causal_f"])
                ve.tensor_copy(upper[:], consts["upper_f"])

        counts = {}
        add_modulation(nc, [(a["c0"], a["wmod0"], mods[0]), (a["c1"], a["wmod1"], mods[1])])

        for k, cfg in enumerate((Cfg(False), Cfg(True))):
            mod = mods[k]
            shift = lambda j, mod=mod: (lambda b: mod[:, j, b:b + 1])
            if upto < 4 * k + 1:
                break
            with nc.sbuf_tensor(f"vall{k}", [P, B * NB, H, QW], F32) as vall:
                with nc.Block() as block:
                    @block.gpsimd
                    def _(pool):
                        pool.memset(vall[:, :, :, 0:DH + 1], 1.0)
                        pool.memset(vall[:, :, :, DH + 1:QW], 0.0)
                if cfg.rel:
                    add_layernorm(nc, f"ln{k}m", xT, hT, shift(1), shift(0), mean_w, eps_col, counts=counts)
                    add_layernorm(nc, f"ln{k}a", hT, hT, lambda b: gb[:, 0:1], lambda b: gb[:, 1:2], mean_w, eps_col, wv=wv[k], bv=bv, vall=vall, counts=counts)
                else:
                    add_layernorm(nc, f"ln{k}a", xT, hT, shift(1), shift(0), mean_w, eps_col, wv=wv[k], vall=vall, counts=counts)
                if upto < 4 * k + 2:
                    break
                add_attention(nc, cfg, xT, hT, vall, mod[:, 2, :], consts,
                              {n: a.get(f"{n}{k}") for n in ("wqk", "wo", "wp", "cols")})
            if upto < 4 * k + 3:
                break
            with nc.sbuf_tensor(f"hhi{k}", [P, NTOK], F32R) as h_hi, nc.sbuf_tensor(f"hlo{k}", [P, NTOK], F32R) as h_lo, \
                    nc.sbuf_tensor(f"CT{k}", [P, NTOK], F32R) as CT:
                add_layernorm(nc, f"ln{k}f", xT, hT, shift(4), shift(3), mean_w, eps_col, dst_hi=h_hi, dst_lo=h_lo, counts=counts)
                add_router(nc, cfg, hT, CT, consts, {n: a[f"{n}{k}"] for n in ("gate", "bias")})
                if upto < 4 * k + 4:
                    break
                add_moe(nc, cfg, xT, h_hi, h_lo, CT, mod[:, 5, :], {"units": a[f"units{k}"]})

        with nc.Block() as block:
            @block.sync
            def _(sp):
                res = hT if upto in (1, 5) else xT
                sp.dma_start(out, res[:]).then_inc(out_done, 16)
                sp.wait_ge(out_done, 16)


def constants():
    ident = np.eye(P)
    i, j = np.arange(P)[:, None], np.arange(P)[None, :]
    causal = np.where(j > i, NEG, 0.0)
    pick = (i == j[:, :HG] * QW + DH).astype(float)
    jd = np.arange(DIAG)[None, :]
    tri = np.concatenate([(jd <= i), (jd >= i + 2)], 1).astype(float)
    div = np.exp(np.arange(0, D, 2, dtype=np.float32) * np.float32(-np.log(10000.0) / D)).astype(np.float64)
    w = np.repeat(div, 2)[:, None]
    odd = (np.arange(D) % 2)[:, None]
    x = np.concatenate([np.arange(T), T + np.arange(T)])[None, :]
    pe = np.where(odd == 1, np.cos(w * x), np.sin(w * x))
    r = np.arange(1, T + 1)[None, :]
    cos, sin = np.cos(w * r), np.sin(w * r) * np.where(odd == 1, -1.0, 1.0)
    row = np.arange(P)[:, None] % QW // DH
    return np.concatenate([ident, causal, pick, tri, pe, cos, sin, -1.0 * (row == 1), -1.0 * (row == 2)], 1).astype(np.float32)


def stacked_columns(w):
    w = w.reshape(w.shape[0], NG, HG, 1, DH)
    z = np.zeros_like(w)
    return np.concatenate([w, w, w, z], 3).reshape(w.shape[0], NG, P).transpose(1, 0, 2)


def selectors(units, up):
    s = np.zeros((units + 2, P, P), np.float32)
    for u in range(units):
        for m in range(P):
            e = u // 2 if up == 2 else 2 * u + m // 64
            s[u + 2, e, m] = s[u + 2, 64 + e, m] = 1.0
    return s


def pack_units(ups, sel, down):
    return np.ascontiguousarray(np.concatenate([*ups, sel, down], 2))


def lay_out(d):
    f = {k: np.asarray(v) for k, v in d.items()}
    a = {"xT": f["L0_attn_x"].reshape(NTOK, D).T, "const": constants(), "ln_gb": np.stack([f["L1_attn_ln_g"], f["L1_attn_ln_b"]], 1)}
    for k in range(2):
        p = f"L{k}_attn_"
        a[f"c{k}"], a[f"wmod{k}"] = f[f"L{k}_c"].T, f[f"L{k}_wmod"]
        a[f"wv{k}"] = f[p + "Wv"]
        a[f"wqk{k}"] = np.concatenate([stacked_columns(f[p + "Wq"]), stacked_columns(f[p + "Wk"])], 2)
        wo = f[p + "Wo"].reshape(NG, HG, DH, D)
        a[f"wo{k}"] = np.concatenate([wo, np.zeros((NG, HG, QW - DH, D), np.float32)], 2).reshape(NG, P, D)
    p = "L1_attn_"
    wp = f[p + "Wp"]
    swapped = wp.reshape(D // 2, 2, D)[:, ::-1].reshape(D, D)
    both = np.stack([stacked_columns(wp), stacked_columns(swapped)])
    both = both.reshape(2, NG, D, HG, QW)
    z = np.zeros((NG, HG, QW, HG, 2, D), np.float32)
    for h in range(HG):
        z[:, h, :, h] = both[:, :, :, h].transpose(1, 3, 0, 2)
    a["wp1"] = z.reshape(NG, P, HG * 2 * D)
    col = lambda v: stacked_columns(v.reshape(1, D))[:, 0, :].T
    a["cols1"] = np.stack([col(f[p + "bq"]), col(f[p + "u_bias"]), col(f[p + "v_bias"]), col(f[p + "bk"]),
                           np.repeat(f[p + "bo"][:, None], NG, 1)], 1)
    a["bv"] = np.broadcast_to(f[p + "bv"], (P, D))
    a["gate0"], a["gate1"] = f["L0_ffn_gate_w"].T, f["L1_ffn_router_w"].T
    a["bias0"] = np.broadcast_to(f["L0_ffn_gate_bias"], (P, 8))
    a["bias1"] = np.broadcast_to(f["L1_ffn_correction_bias"], (P, 64))
    halves = lambda shared, w: np.concatenate([shared[None], w]).reshape(-1, P, D)
    w1, w3 = (halves(f[f"L0_ffn_s{n}"], f[f"L0_ffn_{n}"]).transpose(0, 2, 1) for n in ("w1", "w3"))
    w2 = np.concatenate([f["L0_ffn_sw2"][None], f["L0_ffn_w2"]]).transpose(0, 2, 1).reshape(-1, P, D)
    a["units0"] = pack_units([w1, w3], selectors(16, 2), w2)
    up = f["L1_ffn_up_w"].reshape(32, 2, D, 64).transpose(0, 2, 1, 3).reshape(32, D, P)
    sup = f["L1_ffn_shared_up_w"].reshape(D, 2, P).transpose(1, 0, 2)
    down = f["L1_ffn_down_w"].reshape(32, P, D)
    sdown = f["L1_ffn_shared_down_w"].reshape(2, P, D)
    a["units1"] = pack_units([np.concatenate([sup, up])], selectors(32, 1), np.concatenate([sdown, down]))
    return {k: np.ascontiguousarray(v) for k, v in a.items()}


def kernel(**inputs):
    import concourse.bacc as bacc
    from concourse.bass_utils import run_bass_kernel_spmd

    nc = bacc.Bacc("TRN2", target_bir_lowering=False, num_devices=1)
    arrays = lay_out(inputs)
    aps = {k: nc.dram_tensor(f"in_{k}", v.shape, mybir.dt.from_np(v.dtype), kind="ExternalInput").ap() for k, v in arrays.items()}
    out = nc.dram_tensor("out_xT", (P, NTOK), F32, kind="ExternalOutput").ap()
    build_program(nc, aps, out)
    r = run_bass_kernel_spmd(nc, [{f"in_{k}": v for k, v in arrays.items()}], core_ids=[0])
    return np.ascontiguousarray(r.results[0]["out_xT"].T).reshape(B, T, D)
```

```python
from collections import namedtuple
from contextlib import ExitStack

import numpy as np

import concourse.bass as bass
from concourse import mybir

P = 128
F32 = mybir.dt.float32
F32R = mybir.dt.float32r
BF16 = mybir.dt.bfloat16
U32 = mybir.dt.uint32
ALU = mybir.AluOpType
ACT = mybir.ActivationFunctionType
AX_X = mybir.AxisListType.X

B, T, D = 4, 512, 128
NTOK = B * T
H, DH = 16, 8
HG = 4
NG = H // HG
NIT = B * NG
NB = T // P
DIAG = P + 1
QW = 32
LN_EPS = 1e-5
NEG = -1e30


class Cfg:

    def __init__(self, rel):
        self.rel = rel
        self.scale = float(DH) ** -0.5
        self.E = 64 if rel else 8
        self.up = 1 if rel else 2
        self.units = 32 if rel else 16


def wait_past(eng, sem, value):
    if isinstance(value, int) and value <= 0:
        return
    eng.wait_ge(sem, value)


def add_layernorm(nc, name, src, dst, mul, add, centre, mean_w, ident, eps, counts, dst_hi=None, dst_lo=None, wt=None, wt_out=None, wt_view=lambda ap: ap, wt_bias=None):
    with ExitStack() as ctx:
        sb = lambda n, s, d=F32: ctx.enter_context(nc.sbuf_tensor(f"{name}_{n}", s, d))
        cent_ps = ctx.enter_context(nc.psum_tensor(f"{name}_cent", [P, B, T], F32))
        rstd_ps = ctx.enter_context(nc.psum_tensor(f"{name}_rstd", [P, B, T], F32))
        sq, scaled, norm = (sb(n, [P, B, T]) for n in ("sq", "scaled", "norm"))
        std, rstd = sb("std", [P, B, NB]), sb("rstd_sb", [P, B, NB])
        names = ("centered", "squared", "var_ready", "std_ready", "scaled", "rstd_ready", "rstd_spread", "norm_ready", "out_ready")
        names += (("hi_ready", "lo_ready") if dst_hi is not None else ()) + (("wt_ready",) if wt is not None else ())
        sem, base = {}, {}
        for n in names:
            sem[n], base[n] = counts.setdefault(n, (None, 0))
            if sem[n] is None:
                sem[n] = nc.alloc_semaphore(f"ln_{n}")
            counts[n] = (sem[n], base[n] + B)

        def wait(eng, n, value):
            eng.wait_ge(sem[n], base[n] + value)

        tokens = lambda b: slice(b * T, (b + 1) * T)
        block = ctx.enter_context(nc.Block())

        def wt_ps(b):
            n = wt.shape[1]
            return cent_ps[:, b, 0:NB * n].rearrange("p (t n) -> p t n", n=n)

        @block.tensor
        def _(pe):
            def center(b):
                pe.matmul(cent_ps[:, b, :], centre, src[:, tokens(b)], start=True, stop=True).then_inc(sem["centered"], 1)

            def variance(b):
                wait(pe, "squared", b + 1)
                for t in range(NB):
                    mm = pe.matmul(rstd_ps[:, b, t:t + 1], sq[:, b, t * P:(t + 1) * P], mean_w, start=True, stop=True, skip_group_check=True)
                mm.then_inc(sem["var_ready"], 1)

            def spread(b):
                wait(pe, "rstd_ready", b + 1)
                for t in range(NB):
                    mm = pe.matmul(rstd_ps[:, b, t * P:(t + 1) * P], rstd[:, b, t:t + 1].broadcast_to([P, P]), ident, start=True, stop=True, skip_group_check=True)
                mm.then_inc(sem["rstd_spread"], 1)

            def project(b):
                wait(pe, "out_ready", b + 1)
                for t in range(NB):
                    lo = b * T + t * P
                    mm = pe.matmul(wt_ps(b)[:, t, :], dst[:, lo:lo + P], wt, start=True, stop=True, skip_group_check=True)
                mm.then_inc(sem["wt_ready"], 1)

            center(0)
            center(1)
            for b in range(B):
                if b + 2 < B:
                    center(b + 2)
                variance(b)
                if b > 0:
                    spread(b - 1)
                if b > 1 and wt is not None:
                    project(b - 2)
            spread(B - 1)
            if wt is not None:
                project(B - 2)
                project(B - 1)

        @block.scalar
        def _(act):
            def square(b):
                wait(act, "centered", b + 1)
                act.activation(sq[:, b, :], cent_ps[:, b, :], ACT.Square).then_inc(sem["squared"], 1)

            def root(b):
                wait(act, "var_ready", b + 1)
                act.activation(std[:, b, :], rstd_ps[:, b, 0:NB], ACT.Sqrt, bias=eps[:, 0:1]).then_inc(sem["std_ready"], 1)

            def shift(b):
                wait(act, "norm_ready", b + 1)
                act.activation(dst[:, tokens(b)], norm[:, b, :], ACT.Identity, bias=add(b), scale=1.0).then_inc(sem["out_ready"], 1)

            square(0)
            square(1)
            for b in range(B):
                if b + 2 < B:
                    square(b + 2)
                root(b)
                if b > 0:
                    shift(b - 1)
            shift(B - 1)

        @block.vector
        def _(ve):
            def reciprocal(b):
                wait(ve, "std_ready", b + 1)
                ve.reciprocal(rstd[:, b, :], std[:, b, :]).then_inc(sem["rstd_ready"], 1)

            def scale(b):
                wait(ve, "squared", b + 1)
                ve.tensor_scalar(scaled[:, b, :], cent_ps[:, b, :], mul(b), None, ALU.mult).then_inc(sem["scaled"], 1)

            def high(b):
                wait(ve, "out_ready", b + 1)
                ve.tensor_copy(dst_hi[:, tokens(b)], dst[:, tokens(b)]).then_inc(sem["hi_ready"], 1)

            def read_product(b):
                wait(ve, "wt_ready", b + 1)
                if wt_bias is None:
                    ve.tensor_copy(wt_out(b), wt_view(wt_ps(b)))
                else:
                    ve.tensor_tensor(wt_out(b), wt_view(wt_ps(b)), wt_bias, ALU.add)

            scale(0)
            reciprocal(0)
            for b in range(B):
                if b + 1 < B:
                    scale(b + 1)
                    reciprocal(b + 1)
                wait(ve, "rstd_spread", b + 1)
                wait(ve, "scaled", b + 1)
                ve.tensor_tensor(norm[:, b, :], scaled[:, b, :], rstd_ps[:, b, :], ALU.mult).then_inc(sem["norm_ready"], 1)
                if dst_hi is not None and b > 0:
                    high(b - 1)
                if wt is not None and b > 1:
                    read_product(b - 2)
            if dst_hi is not None:
                high(B - 1)
            if wt is not None:
                read_product(B - 2)
                read_product(B - 1)

        @block.gpsimd
        def _(pool):
            if dst_lo is not None:
                for b in range(B):
                    wait(pool, "hi_ready", b + 1)
                    pool.tensor_tensor(dst_lo[:, tokens(b)], dst[:, tokens(b)], dst_hi[:, tokens(b)].bitcast(F32), ALU.subtract).then_inc(sem["lo_ready"], 1)


def add_modulation(nc, layers, start_sync, start_vector, start_gpsimd):
    with ExitStack() as ctx:
        sem = lambda n: nc.alloc_semaphore(f"mod_{n}")
        loaded, silu_ready, made, copied, step = sem("ld"), sem("silu"), sem("mm"), sem("cp"), sem("step")
        tiles = []
        for k, (cT, wmod, mod) in enumerate(layers):
            tiles.append((
                ctx.enter_context(nc.sbuf_tensor(f"mod_c{k}", [P, B], F32)),
                ctx.enter_context(nc.sbuf_tensor(f"mod_s{k}", [P, B], F32)),
                ctx.enter_context(nc.sbuf_tensor(f"mod_w{k}", [P, 6 * D], F32)),
                ctx.enter_context(nc.sbuf_tensor(f"mod_sg{k}", [P, 2, B], F32)),
                ctx.enter_context(nc.sbuf_tensor(f"mod_mg{k}", [P, 2, B], F32)),
                ctx.enter_context(nc.psum_tensor(f"mod_p{k}", [P, 6, B], F32)),
            ))
        n = len(layers)
        block = ctx.enter_context(nc.Block())

        @block.sync
        def _(sp):
            for (cT, wmod, _), t in zip(layers, tiles):
                sp.dma_start(t[0][:], cT).then_inc(loaded, 16)
                sp.dma_start(t[2][:], wmod).then_inc(loaded, 16)
            start_sync(sp)

        @block.gpsimd
        def _(pool):
            start_gpsimd(pool)

        @block.scalar
        def _(act):
            act.wait_ge(loaded, 32 * n)
            for t in tiles:
                act.activation(t[1][:], t[0][:], ACT.Silu).then_inc(silu_ready, 1)

        @block.tensor
        def _(pe):
            pe.wait_ge(silu_ready, n)
            for t in tiles:
                for k in range(6):
                    mm = pe.matmul(t[5][:, k, :], t[2][:, k * D:(k + 1) * D], t[1][:], start=True, stop=True)
                mm.then_inc(made, 1)

        @block.vector
        def _(ve):
            start_vector(ve)
            for k, ((_, _, mod), t) in enumerate(zip(layers, tiles)):
                ve.wait_ge(made, k + 1)
                ve.tensor_copy(mod[:], t[5][:]).then_inc(copied, 1)
                ve.wait_ge(copied, k + 1)
                sg, mg = t[3], t[4]
                gates = mod[:, 2::3, :]
                gains = mod[:, 1::3, :]
                ve.tensor_scalar(sg[:], gates, 0.0, 2.0, ALU.is_ge, ALU.mult).then_inc(step, 1)
                ve.tensor_scalar(mg[:], gates, -1.0, None, ALU.mult).then_inc(step, 1)
                ve.tensor_scalar(gains, gains, 1.0, None, ALU.add).then_inc(step, 1)
                ve.wait_ge(step, 5 * k + 3)
                ve.scalar_tensor_tensor(out=mg[:], in0=mg[:], scalar=0.25, in1=gates, op0=ALU.max, op1=ALU.max).then_inc(step, 1)
                ve.wait_ge(step, 5 * k + 4)
                ve.scalar_tensor_tensor(out=gates, in0=sg[:], scalar=-1.0, in1=mg[:], op0=ALU.add, op1=ALU.mult).then_inc(step, 1)


def add_attention(nc, cfg, xT, hT, vall, qz, diag, wp_all, wp_all_loaded, gate, consts, dram):
    rel = cfg.rel
    name = "rel" if rel else "cau"
    with ExitStack() as ctx:
        sb = lambda n, s, d=F32: ctx.enter_context(nc.sbuf_tensor(f"{name}_{n}", s, d))
        sem = lambda n: nc.alloc_semaphore(f"{name}_{n}")
        ps = ctx.enter_context(nc.psum_tensor(f"{name}_ps", [P, 8, T], F32))
        S = lambda i: ps[:, i, :]
        BANK_A, BANK_B, BANK_T = ps[:, 4, :], ps[:, 5, :], lambda j: ps[:, 6 + j % 2, :]

        wqk = sb("wqk", [P, 2, P])
        wo = sb("wo", [P, P])
        vcur = sb("vcur", [P, NB, HG, QW])
        qs, ks = sb("qs", [P, T]), sb("ks", [P, T])
        q_hi, k_hi = sb("qhi", [P, T], F32R), sb("khi", [P, T], F32R)
        qst = sb("qst", [P, T], F32R)
        kst = [sb(f"kst{p}", [P, T], F32R) for p in range(2)]
        probs = sb("probs", [P, 2, NB, T])
        negmax = sb("negmax", [P, HG, NB])
        pT = sb("pT", [P, HG, NB, T])
        o_sb, o_norm = sb("o", [P, T]), sb("onorm", [P, T])
        recip, spread = sb("recip", [P, NB * HG]), sb("spread", [P, NB * HG, QW])
        if rel:
            as_, a_hi, ast = sb("as", [P, T]), sb("ahi", [P, T], F32R), sb("ast", [P, T], F32R)
            wp_hi = sb("wphi", [P, HG * 2 * P], F32R)
            wp = sb("wp", [P, HG, 2, P], F32R)
            rot1, rot2 = sb("rot1", [P, T]), sb("rot2", [P, T])
            gT = sb("gT", [P, 2, T + 1])
            cols = sb("cols", [P, 5, NG])
            bqu, bqv, bks = sb("bqu", [P, NG]), sb("bqv", [P, NG]), sb("bks", [P, NG])
            gbo = sb("gbo", [P, B])

        wqk_loaded, wo_loaded, v_loaded = sem("wqk"), sem("wo"), sem("v")
        proj_ready, q_scaled, rounded = sem("proj"), sem("qsc"), sem("rnd")
        q_stacked, k_stacked = sem("qst"), sem("kst")
        placed = [sem("pl0"), sem("pl1")]
        scores_ready, max_ready, exp_ready = sem("sc"), sem("mx"), sem("exp")
        turned, copied_by_act, copied_by_dve = sem("tr"), sem("tra"), sem("trv")
        pv_ready, o_copied, sums_ready, recip_ready = sem("pv"), sem("oc"), sem("sum"), sem("rec")
        recip_spread, spread_ready, o_normed = sem("rsp"), sem("spr"), sem("on")
        wo_done, x_added = sem("wod"), sem("xa")
        if rel:
            wp_loaded, once, bias_step = sem("wp"), sem("once"), sem("bst")
            g_ready, rotated, g_summed, a_stacked = sem("g"), sem("rot"), sem("gs"), sem("ast")
            lu_ready, lower_masked, diag_masked = sem("lu"), sem("lm"), sem("dm")
            wp_split, wp_rounded = sem("wps"), sem("wpr")
        ve_passed, pool_passed = sem("vep"), sem("pop")
        PLACED = 16 * HG
        NPROJ = 2 + rel
        BANK_O, BANK_R = (BANK_T(1), BANK_T(0)) if rel else (BANK_A, BANK_B)
        DVE_COPIES = () if rel else (1,)
        ACT_COPIES = tuple(j for j in range(NB) if j not in DVE_COPIES)
        NCA, NCV = len(ACT_COPIES), len(DVE_COPIES)

        if rel:
            with nc.Block() as setup:
                @setup.sync
                def _(sp):
                    sp.dma_start(cols[:], dram["cols"]).then_inc(once, 16)

                @setup.gpsimd
                def _(pool):
                    pool.memset(gT[:, :, T:T + 1], 0.0)

                @setup.vector
                def _(ve):
                    ve.wait_ge(wp_all_loaded, 16)
                    for g in range(NG):
                        raw = wp_all[:, g, :].bitcast(F32)
                        wait_past(ve, wp_split, g)
                        ve.tensor_copy(wp_hi[:], raw).then_inc(wp_rounded, 1)
                        ve.wait_ge(wp_rounded, g + 1)
                        ve.scalar_tensor_tensor(out=wp_all[:, g, :], in0=wp_hi[:].bitcast(F32), scalar=consts["neg_lo_k"],
                                                in1=raw, op0=ALU.mult, op1=ALU.add).then_inc(wp_split, 1)
                    ve.wait_ge(once, 16)
                    ve.tensor_tensor(rot1[:, 0:NG], cols[:, 0, :], cols[:, 1, :], ALU.add).then_inc(bias_step, 1)
                    ve.tensor_tensor(rot2[:, 0:NG], cols[:, 0, :], cols[:, 2, :], ALU.add).then_inc(bias_step, 1)
                    ve.tensor_scalar(gbo[:], gate, cols[:, 4, 0:1], None, ALU.mult).then_inc(bias_step, 1)
                    ve.tensor_copy(bks[:], cols[:, 3, :])
                    ve.wait_ge(bias_step, 3)
                    ve.tensor_scalar(bqu[:], rot1[:, 0:NG], cfg.scale, None, ALU.mult)
                    ve.tensor_scalar(bqv[:], rot2[:, 0:NG], cfg.scale, None, ALU.mult)
                    for b in range(B):
                        s = slice(b * T, (b + 1) * T)
                        ve.tensor_scalar(xT[:, s], xT[:, s], gbo[:, b:b + 1], None, ALU.add)

        block = ctx.enter_context(nc.Block())

        def loop(eng, body):
            def two(m):
                for p in range(2):
                    body(2 * m + p, p, isinstance(m, int) and 2 * m + p == NIT - 1)

            two(0)
            with eng.Fori(1, NIT // 2 - 1) as m:
                two(m)
            two(NIT // 2 - 1)

        def wait_copied(eng, head, j):
            if j in DVE_COPIES:
                wait_past(eng, copied_by_dve, NCV * head + DVE_COPIES.index(j) + 1)
            else:
                wait_past(eng, copied_by_act, NCA * head + ACT_COPIES.index(j) + 1)

        @block.sync
        def _(sp):
            def load_wqk(n):
                wait_past(sp, proj_ready, 2 * n)
                sp.dma_start(wqk[:], dram["wqk"][bass.ds(n % NG, 1)].rearrange("o p (k m) -> p (o k) m", k=2)).then_inc(wqk_loaded, 16)

            def load_wp(n):
                wait_past(sp, g_ready, HG * n)
                sp.dma_start(wp[:].bitcast(F32), wp_all[:, bass.ds(n % NG, 1), :].bitcast(F32).rearrange(
                    "p o (h k m) -> p (o h) k m", h=HG, k=2)).then_inc(wp_loaded, 16)

            def place_queries(n, p):
                sp.wait_ge(q_stacked, n + 1)
                for h in range(HG):
                    r = slice(h * QW, (h + 1) * QW)
                    sp.dma_start(qz[p][r, h, :].bitcast(F32), qst[r, :].bitcast(F32)).then_inc(placed[p], 16)

            def body(n, p, last):
                wait_past(sp, pv_ready, n)
                sp.dma_start(vcur[:], vall[:, bass.ds((n // NG) * NB, NB), bass.ds((n % NG) * HG, HG), :]).then_inc(v_loaded, 16)
                if not (isinstance(n, int) and n + 2 >= NIT):
                    load_wqk(n + 2)
                if not rel and not last:
                    place_queries(n + 1, 1 - p)
                wait_past(sp, wo_done, n)
                sp.dma_start(wo[:], dram["wo"][bass.ds(n % NG, 1)].rearrange("o p m -> p (o m)")).then_inc(wo_loaded, 16)
                if rel and not last:
                    load_wp(n + 1)
                    place_queries(n + 1, 1 - p)

            load_wqk(0)
            if rel:
                load_wp(0)
            load_wqk(1)
            place_queries(0, 0)
            loop(sp, body)

        @block.tensor
        def _(pe):
            def project(n):
                pe.wait_ge(wqk_loaded, 16 * (n + 1))
                wait_past(pe, q_scaled, NPROJ * n)
                if rel and not (isinstance(n, int) and n == 0):
                    pe.wait_ge(rotated, 2 * (HG * (n - 1) + 3))
                elif not rel:
                    wait_past(pe, x_added, n - 2)
                batch = hT[:, bass.ds((n // NG) * T, T)]
                pe.matmul(BANK_A, wqk[:, 0, :], batch, start=True, stop=True).then_inc(proj_ready, 1)
                pe.matmul(BANK_B, wqk[:, 1, :], batch, start=True, stop=True).then_inc(proj_ready, 1)

            def frequencies(n, h):
                if h == 0:
                    pe.wait_ge(wp_loaded, 16 * (n + 1))
                    pe.wait_ge(a_stacked, n + 1)
                    pe.wait_ge(q_scaled, NPROJ * (n + 1))
                wait_past(pe, diag_masked, HG * NB * n + NB * h)
                pe.matmul(BANK_A, wp[:, h, 0, :], ast[:], start=True, stop=True)
                pe.matmul(BANK_B, wp[:, h, 1, :], ast[:], start=True, stop=True).then_inc(g_ready, 1)

            def diagonal(n, h, i, last=False):
                if i == 0:
                    pe.wait_ge(g_summed, HG * n + h + 1)
                    if h == 2 and not last:
                        pe.wait_ge(q_scaled, NPROJ * (n + 2))
                if i >= 2:
                    pe.wait_ge(diag_masked, HG * NB * n + NB * h + i - 1)
                d, w = i * P, min(DIAG, T - i * P)
                bank, g = ps[:, 4 + i % 2, :], gT[:, h % 2, :]
                pe.matmul(bank[:, 0:w], g[:, d:d + P], consts["pe"][:, T + d:T + d + w], start=True, stop=True,
                          skip_group_check=True)
                pe.matmul(bank[:, DIAG:DIAG + w], g[:, d + 1:d + P + 1], consts["pe"][:, d:d + w], start=True, stop=True,
                          skip_group_check=True).then_inc(lu_ready, 1)

            def scores(n, p, h, i):
                base = HG * NB * n + NB * h
                if h == 0 and i == 0:
                    pe.wait_ge(placed[p], PLACED // 2 * (n - p) + PLACED)
                    pe.wait_ge(k_stacked, n + 1)
                wait_past(pe, exp_ready, base + i + 1 - NB)
                d, e = i * P, (i + 1) * P
                q, k = qz[p][:, h, d:e], kst[p]
                if not rel:
                    w = max(e, 2 * P)
                    pe.matmul(S(i)[:, 0:w], q, k[:, 0:w], start=True, stop=False, skip_group_check=True)
                    pe.matmul(S(i)[:, d:e], consts["ident_bf"], consts["causal"], start=False, stop=True,
                              skip_group_check=True).then_inc(scores_ready, 1)
                    return
                g = gT[:, h % 2, :]
                mm = pe.matmul(S(i), q, k[:], start=True, stop=False, skip_group_check=True)
                if i > 0:
                    mm = pe.matmul(S(i)[:, 0:d], g[:, d:e], consts["pe"][:, T:T + d], start=False, stop=False, skip_group_check=True)
                if i < NB - 1:
                    mm = pe.matmul(S(i)[:, e + 1:T], g[:, d + 1:e + 1], consts["pe"][:, e + 1:T], start=False, stop=False,
                                   skip_group_check=True)
                mm.then_inc(scores_ready, 1)

            def transposes(n, h, j):
                base = HG * NB * n + NB * h
                pe.wait_ge(exp_ready, base + NB)
                wait_copied(pe, HG * n + h - (j < 2), (j - 2) % NB)
                if rel and h == 0 and j < 2:
                    wait_past(pe, (o_normed, x_added)[j], n)
                for i in range(0 if rel else j, NB):
                    tr = pe.transpose(BANK_T(j)[:, i * P:(i + 1) * P], probs[:, h % 2, i, j * P:(j + 1) * P], consts["ident"])
                tr.then_inc(turned, 1)

            def values(n, last=False):
                wait_copied(pe, HG * n + HG - 1, ACT_COPIES[-1])
                if DVE_COPIES:
                    wait_copied(pe, HG * n + HG - 1, DVE_COPIES[-1])
                if not rel and not last:
                    pe.wait_ge(q_scaled, NPROJ * (n + 3))
                if not rel:
                    wait_past(pe, x_added, n)
                pe.wait_ge(v_loaded, 16 * (n + 1))
                for j in range(NB):
                    i0 = 0 if rel else j * P
                    for h in range(HG):
                        mm = pe.matmul(BANK_O[h * QW:(h + 1) * QW, i0:T], vcur[:, j, h, :], pT[:, h, j, i0:T],
                                       start=(j == 0), stop=(j == NB - 1), skip_group_check=True)
                mm.then_inc(pv_ready, 1)

            def sums(n):
                pe.wait_ge(o_copied, n + 1)
                for i in range(NB):
                    mm = pe.matmul(BANK_R[:, i * HG:(i + 1) * HG], o_sb[:, i * P:(i + 1) * P], consts["pick"],
                                   start=True, stop=True, skip_group_check=True)
                mm.then_inc(sums_ready, 1)

            def spread_recips(n):
                pe.wait_ge(recip_spread, n + 1)
                for i in range(NB):
                    mm = pe.matmul(BANK_R[:, i * P:(i + 1) * P], spread[:, i * HG:(i + 1) * HG, :].rearrange("p h q -> p (h q)"),
                                   consts["ident"], start=True, stop=True, skip_group_check=True)
                mm.then_inc(spread_ready, 1)

            def project_out(n):
                pe.wait_ge(o_normed, n + 1)
                pe.wait_ge(wo_loaded, 16 * (n + 1))
                pe.matmul(BANK_O, wo[:], o_norm[:], start=True, stop=True).then_inc(wo_done, 1)

            def body(n, p, last):
                first = isinstance(n, int) and n == 0
                for h in range(HG):
                    before = (n - 1, HG - 1) if h == 0 else (n, h - 1)
                    after = (n + 1, 0) if h == HG - 1 else (n, h + 1)
                    turn = h > 0 or not first
                    tail = not first and h == 1
                    if rel:
                        diagonal(n, h, 0, last)
                        diagonal(n, h, 1)
                        scores(n, p, h, 0)
                        if tail:
                            values(n - 1, last)
                        diagonal(n, h, 2)
                        diagonal(n, h, 3)
                        scores(n, p, h, 1)
                        if tail:
                            sums(n - 1)
                        elif turn and h != 1:
                            transposes(*before, 0)
                        if not (h == HG - 1 and last):
                            frequencies(*after)
                        scores(n, p, h, 2)
                        if tail:
                            spread_recips(n - 1)
                        elif turn and h != 1:
                            transposes(*before, 1)
                        if h == 1 and not last:
                            project(n + 1)
                        scores(n, p, h, 3)
                        if tail:
                            project_out(n - 1)
                        for j in range(0 if h == 1 else 2, NB):
                            if turn:
                                transposes(*before, j)
                    else:
                        for j in range(NB):
                            if turn:
                                transposes(*before, j)
                            if j % 2 and not (h == HG - 1 and last):
                                for i in (j - 1, j):
                                    scores(after[0], 1 - p if h == HG - 1 else p, after[1], i)
                        if h == 0:
                            if not last:
                                project(n + 1)
                            if not first:
                                values(n - 1, last)
                        elif not first:
                            (sums, spread_recips, project_out)[h - 1](n - 1)

            project(0)
            if rel:
                frequencies(0, 0)
            else:
                for i in range(NB):
                    scores(0, 0, 0, i)
            loop(pe, body)
            for j in range(NB):
                transposes(NIT - 1, HG - 1, j)
            values(NIT - 1, True)
            sums(NIT - 1)
            spread_recips(NIT - 1)
            project_out(NIT - 1)

        @block.scalar
        def _(act):
            def read(dst, bank, bias, scale):
                if bias is None:
                    ins = act.activation(dst[:], bank, ACT.Copy, scale=scale)
                else:
                    ins = act.activation(dst[:], bank, ACT.Identity, bias=bias, scale=scale)
                ins.then_inc(q_scaled, 1)

            def read_projections(n):
                g = n % NG
                act.wait_ge(proj_ready, 2 * n + 1)
                wait_past(act, q_stacked, n)
                wait_past(act, k_stacked, n)
                if rel:
                    wait_past(act, a_stacked, n)
                    read(as_, BANK_A, bqv[:, bass.ds(g, 1)], cfg.scale)
                read(qs, BANK_A, bqu[:, bass.ds(g, 1)] if rel else None, cfg.scale)
                act.wait_ge(proj_ready, 2 * n + 2)
                read(ks, BANK_B, bks[:, bass.ds(g, 1)] if rel else None, 1.0)

            def exp(n, h, i):
                base = HG * NB * n + NB * h
                if i == 0:
                    wait_past(act, turned, base - NB)
                w = T if rel else (i + 1) * P
                act.wait_ge(max_ready, base + i + 1)
                act.activation(probs[:, h % 2, i, 0:w], S(i)[:, 0:w], ACT.Exp, bias=negmax[:, h, i:i + 1],
                               scale=-1.0 if rel else 1.0).then_inc(exp_ready, 1)

            def copy(n, h, j):
                if h == 0 and j == ACT_COPIES[0]:
                    wait_past(act, pv_ready, n)
                i0 = 0 if rel else j * P
                act.wait_ge(turned, HG * NB * n + NB * h + j + 1)
                act.copy(pT[:, h, j, i0:T], BANK_T(j)[:, i0:T]).then_inc(copied_by_act, 1)

            def copy_values(n):
                act.wait_ge(pv_ready, n + 1)
                wait_past(act, o_normed, n)
                act.copy(o_sb[:], BANK_O).then_inc(o_copied, 1)

            def body(n, p, last):
                first = isinstance(n, int) and n == 0
                for h in range(HG):
                    before = (n - 1, HG - 1) if h == 0 else (n, h - 1)
                    turn = h > 0 or not first
                    after_exp = {1: (0, 1), 2: (2,), 3: (3,)} if rel else {2: (0,), 3: (2, 3)}
                    if rel and h == 1:
                        after_exp = {3: (0, 1, 2, 3)}
                    for i in range(NB):
                        if rel and i == 3 and h == 1 and not last:
                            read_projections(n + 1)
                        exp(n, h, i)
                        if h == 1 and i == (0 if rel else 2) and not first:
                            copy_values(n - 1)
                        for j in after_exp.get(i, ()):
                            if turn and j in ACT_COPIES:
                                copy(*before, j)
                    if not rel and h == 0 and not last:
                        read_projections(n + 1)

            read_projections(0)
            loop(act, body)
            for j in ACT_COPIES:
                copy(NIT - 1, HG - 1, j)
            copy_values(NIT - 1)

        @block.vector
        def _(ve):
            def stack_queries(n, p):
                ve.wait_ge(rounded, NPROJ * n + NPROJ - 1)
                wait_past(ve, scores_ready, HG * NB * (n - 1))
                wait_past(ve, placed[1 - p], PLACED // 2 * (n + p))
                ve.scalar_tensor_tensor(out=qst[:], in0=q_hi[:].bitcast(F32), scalar=consts["neg_lo_q"],
                                        in1=qs[:], op0=ALU.mult, op1=ALU.add).then_inc(q_stacked, 1)

            def stack_keys(n, p):
                ve.wait_ge(rounded, NPROJ * (n + 1))
                wait_past(ve, scores_ready, HG * NB * (n - 1))
                ve.scalar_tensor_tensor(out=kst[p][:], in0=k_hi[:].bitcast(F32), scalar=consts["neg_lo_k"],
                                        in1=ks[:], op0=ALU.mult, op1=ALU.add).then_inc(k_stacked, 1)

            def stack_positions(n):
                ve.wait_ge(rounded, NPROJ * n + 1)
                wait_past(ve, g_ready, HG * n)
                ve.scalar_tensor_tensor(out=ast[:], in0=a_hi[:].bitcast(F32), scalar=consts["neg_lo_q"],
                                        in1=as_[:], op0=ALU.mult, op1=ALU.add).then_inc(a_stacked, 1)

            def copy(n, h, j):
                wait_past(ve, pv_ready, n)
                i0 = 0 if rel else j * P
                ve.wait_ge(turned, HG * NB * n + NB * h + j + 1)
                ve.tensor_copy(pT[:, h, j, i0:T], BANK_T(j)[:, i0:T]).then_inc(copied_by_dve, 1)

            def rotate(n, h):
                ve.wait_ge(g_ready, HG * n + h + 1)
                wait_past(ve, g_summed, HG * n + h)
                ve.tensor_tensor(rot1[:], BANK_A, consts["cos"], ALU.mult).then_inc(rotated, 1)
                ve.tensor_tensor(rot2[:], BANK_B, consts["sin"], ALU.mult).then_inc(rotated, 1)

            def mask(n, h, i):
                base = HG * NB * n + NB * h
                w = min(DIAG, T - i * P)
                d, bank = slice(i * P, i * P + w), ps[:, 4 + i % 2, :]
                ve.wait_ge(lu_ready, base + i + 1)
                wait_past(ve, max_ready, base + i + 1 - NB)
                ve.tensor_tensor(diag[:, i, d], bank[:, 0:w], consts["lower"][:, 0:w], ALU.mult).then_inc(lower_masked, 1)
                ve.wait_ge(lower_masked, base + i + 1)
                ve.sem_inc(ve_passed, 1)
                ve.copy_predicated(diag[:, i, d], consts["upper"][:, 0:w], bank[:, DIAG:DIAG + w]).then_inc(diag_masked, 1)

            def maximum(n, h, i):
                base = HG * NB * n + NB * h
                ve.wait_ge(scores_ready, base + i + 1)
                if i == 0:
                    wait_past(ve, exp_ready, base + NB - HG * NB)
                if rel:
                    ve.wait_ge(diag_masked, base + i + 1)
                    ve.sem_inc(ve_passed, 1)
                    ve.tensor_tensor_reduce(S(i), S(i), diag[:, i, :], -1.0, -NEG, ALU.add, ALU.min,
                                            negmax[:, h, i:i + 1]).then_inc(max_ready, 1)
                else:
                    ve.tensor_reduce(negmax[:, h, i:i + 1], S(i)[:, 0:(i + 1) * P], AX_X, ALU.max, negate=True).then_inc(max_ready, 1)

            def reciprocals(n):
                ve.wait_ge(sums_ready, n + 1)
                ve.reciprocal(recip[:], BANK_R[:, 0:NB * HG]).then_inc(recip_ready, 1)
                ve.wait_ge(recip_ready, n + 1)
                wait_past(ve, spread_ready, n)
                ve.tensor_copy(spread[:], recip[:].unsqueeze(2).broadcast_to([P, NB * HG, QW])).then_inc(recip_spread, 1)

            def normalise(n):
                ve.wait_ge(spread_ready, n + 1)
                wait_past(ve, wo_done, n)
                ve.tensor_tensor(o_norm[:], o_sb[:], BANK_R, ALU.mult).then_inc(o_normed, 1)

            def add_to_x(n):
                ve.wait_ge(wo_done, n + 1)
                s = bass.ds((n // NG) * T, T)
                ve.scalar_tensor_tensor(out=xT[:, s], in0=BANK_O, scalar=gate[:, bass.ds(n // NG, 1)],
                                        in1=xT[:, s], op0=ALU.mult, op1=ALU.add).then_inc(x_added, 1)

            def body(n, p, last):
                first = isinstance(n, int) and n == 0
                for h in range(HG):
                    before = (n - 1, HG - 1) if h == 0 else (n, h - 1)
                    after = (n + 1, 0) if h == HG - 1 else (n, h + 1)
                    tail = not first and h == 1
                    stack = not last
                    if rel:
                        mask(n, h, 0)
                        mask(n, h, 1)
                        maximum(n, h, 0)
                        mask(n, h, 2)
                        mask(n, h, 3)
                        maximum(n, h, 1)
                        if tail:
                            reciprocals(n - 1)
                        if not (h == HG - 1 and last):
                            rotate(*after)
                        maximum(n, h, 2)
                        if tail:
                            normalise(n - 1)
                        maximum(n, h, 3)
                        if tail:
                            add_to_x(n - 1)
                        if stack and h == 2:
                            stack_positions(n + 1)
                            stack_queries(n + 1, 1 - p)
                        if stack and h == 3:
                            stack_keys(n + 1, 1 - p)
                    else:
                        if h > 0 or not first:
                            copy(*before, 1)
                        if h == 0 and not (isinstance(n, int) and n < 2):
                            add_to_x(n - 2)
                        if stack and h == 1:
                            stack_queries(n + 1, 1 - p)
                        if h == 2 and not first:
                            reciprocals(n - 1)
                        if h == 3 and not first:
                            normalise(n - 1)
                        if not (h == HG - 1 and last):
                            for i in range(NB):
                                maximum(*after, i)
                        if stack and h == 2:
                            stack_keys(n + 1, 1 - p)

            if rel:
                stack_positions(0)
            stack_queries(0, 0)
            stack_keys(0, 0)
            if rel:
                rotate(0, 0)
            else:
                for i in range(NB):
                    maximum(0, 0, i)
            loop(ve, body)
            for j in DVE_COPIES:
                copy(NIT - 1, HG - 1, j)
            if not rel:
                add_to_x(NIT - 2)
            reciprocals(NIT - 1)
            normalise(NIT - 1)
            add_to_x(NIT - 1)

        @block.gpsimd
        def _(pool):
            def high(n, k, dst, src):
                pool.wait_ge(q_scaled, NPROJ * n + k + 1)
                wait_past(pool, k_stacked if k == NPROJ - 1 else q_stacked, n)
                if rel and k == 0:
                    wait_past(pool, a_stacked, n)
                pool.sem_inc(pool_passed, 1)
                pool.tensor_copy(dst[:], src[:]).then_inc(rounded, 1)

            def high_queries(n):
                if rel:
                    high(n, 0, a_hi, as_)
                high(n, NPROJ - 2, q_hi, qs)

            def high_keys(n):
                high(n, NPROJ - 1, k_hi, ks)

            def sum_rotated(n, h):
                pool.wait_ge(rotated, 2 * (HG * n + h + 1))
                wait_past(pool, scores_ready, HG * NB * n + NB * (h - 1))
                pool.tensor_tensor(gT[:, h % 2, 0:T], rot1[:], rot2[:], ALU.add).then_inc(g_summed, 1)

            def body(n, p, last):
                for h in range(HG):
                    if rel and not (h == HG - 1 and last):
                        sum_rotated(*((n + 1, 0) if h == HG - 1 else (n, h + 1)))
                    if h == (1 if rel else 0) and not last:
                        high_queries(n + 1)
                    if h == (2 if rel else 0) and not last:
                        high_keys(n + 1)

            high_queries(0)
            high_keys(0)
            if rel:
                sum_rotated(0, 0)
            loop(pool, body)


Router = namedtuple("Router", "load zero turn activate copy_turned choose ready")


def make_router(nc, ctx, cfg, logits, CT, turned_bank, consts, dram):
    E, NT, name = cfg.E, NTOK // P, "r1" if cfg.rel else "r0"
    G, GE = 8, 8
    BIG = 3e38
    sb = lambda n, s, d=F32: ctx.enter_context(nc.sbuf_tensor(f"{name}_{n}", s, d))
    sem = lambda n: nc.alloc_semaphore(f"{name}_{n}")
    bias = sb("bias", [P, E])
    score, biased, rep = sb("score", [P, NT, E]), sb("biased", [P, NT, E]), sb("rep", [P, NT, E])
    v8, red, rcp = sb("v8", [P, NT, 8]), sb("red", [P, NT]), sb("rcp", [P, NT])
    sel, comb = sb("sel", [P, NT, E]), sb("comb", [P, NT, E])
    stack = sb("stack", [P, NT, P], F32R)
    if cfg.rel:
        masked = sb("masked", [P, NT, E])
        gmask = sb("gmask", [P, NT, G], U32)
        emask = sb("emask", [P, NT * G, GE], U32)
        hi1, lo1 = (sb(n, [P, NT * G, 4]) for n in ("hi1", "lo1"))
        hi2, lo2, t1, t2 = (sb(n, [P, NT * G, 2]) for n in ("hi2", "lo2", "t1", "t2"))
        gs, grep = sb("gs", [P, NT, G]), sb("grep", [P, NT, G])
    loaded, act_ready, step = sem("ld"), sem("act"), sem("st")
    stacked, turned, in_ready, ready = sem("stk"), sem("tr"), sem("in"), sem("ct")

    def over_experts(a):
        return a.unsqueeze(2).broadcast_to([P, NT, E])

    def load(sp):
        sp.dma_start(bias[:], dram["bias"]).then_inc(loaded, 16)

    def zero(pool):
        pool.memset(stack[:].bitcast(F32), 0.0).then_inc(in_ready, 1)
        if cfg.rel:
            pool.memset(masked[:], 0.0).then_inc(in_ready, 1)

    def turn(pe):
        pe.wait_ge(stacked, 2)
        for t in range(NT):
            if t % NB == 0:
                wait_past(pe, ready, t // NB - 1)
            tr = pe.transpose(turned_bank(t // NB)[:, (t % NB) * P:(t % NB + 1) * P], stack[:, t, :].bitcast(F32), consts["ident"])
            if t % NB == NB - 1:
                tr.then_inc(turned, 1)

    def activate(act):
        if cfg.rel:
            act.activation(score[:], logits[:], ACT.Sigmoid).then_inc(act_ready, 1)
        else:
            act.wait_ge(step, 2)
            act.activation(rep[:], biased[:], ACT.Exp).then_inc(act_ready, 1)

    def copy_turned(act):
        for b in range(B):
            act.wait_ge(turned, b + 1)
            act.copy(CT[:, b * T:(b + 1) * T], turned_bank(b)).then_inc(ready, 1)

    def choose(ve):
        done = [0]

        def chain(ins):
            done[0] += 1
            ins.then_inc(step, 1)
            ve.wait_ge(step, done[0])

        ve.wait_ge(loaded, 16)
        ve.wait_ge(in_ready, 1 + cfg.rel)
        if not cfg.rel:
            chain(ve.tensor_reduce(red[:], logits[:], AX_X, ALU.max))
            chain(ve.tensor_tensor(biased[:], logits[:], over_experts(red[:]), ALU.subtract))
            ve.wait_ge(act_ready, 1)
            chain(ve.reduce_sum(red[:], rep[:], AX_X))
            chain(ve.reciprocal(rcp[:], red[:]))
            chain(ve.tensor_tensor(score[:], rep[:], over_experts(rcp[:]), ALU.mult))
        else:
            ve.wait_ge(act_ready, 1)
        bias_all = bias[:].unsqueeze(1).broadcast_to([P, NT, E])
        chain(ve.tensor_tensor(biased[:], score[:], bias_all, ALU.add))

        def pick_top(out, values, k):
            for t in range(NT):
                ins = ve.max(v8[:, t, :], values[:, t, :])
            chain(ins)
            if k < 8:
                chain(ve.memset(v8[:, :, k:8], BIG))
            for t in range(NT):
                ins = ve.match_replace(out[:, t, :], v8[:, t, :], values[:, t, :], -BIG)
            chain(ins)

        if not cfg.rel:
            pick_top(rep[:], biased[:], 2)
            chain(ve.scalar_tensor_tensor(out=comb[:], in0=rep[:], scalar=-1e38, in1=score[:], op0=ALU.is_le, op1=ALU.mult))
        else:
            def pairs(a, n):
                v = a.rearrange("p g (n two) -> p g n two", two=2)
                return v[:, :, :, 0], v[:, :, :, 1]

            v = biased[:].rearrange("p t (g e) -> p (t g) e", e=GE)
            a, b_ = pairs(v, 4)
            chain(ve.tensor_tensor(hi1[:], a, b_, ALU.max))
            chain(ve.tensor_tensor(lo1[:], a, b_, ALU.min))
            w, hi, lo, hi_next, lo_next = 4, hi1, lo1, hi2, lo2
            while w > 1:
                ha, hb = pairs(hi[:, :, 0:w], w // 2)
                la, lb = pairs(lo[:, :, 0:w], w // 2)
                u = w // 2
                chain(ve.tensor_tensor(t1[:, :, 0:u], ha, hb, ALU.min))
                chain(ve.tensor_tensor(t2[:, :, 0:u], la, lb, ALU.max))
                chain(ve.tensor_tensor(lo_next[:, :, 0:u], t1[:, :, 0:u], t2[:, :, 0:u], ALU.max))
                chain(ve.tensor_tensor(hi_next[:, :, 0:u], ha, hb, ALU.max))
                w, hi, lo, hi_next, lo_next = u, hi_next, lo_next, hi, lo
            chain(ve.tensor_tensor(gs[:].rearrange("p t g -> p (t g)"), hi[:, :, 0], lo[:, :, 0], ALU.add))
            pick_top(grep[:], gs[:], 4)
            chain(ve.tensor_scalar(gmask[:], grep[:], -1e38, None, ALU.is_le))
            chain(ve.tensor_copy(emask[:], gmask[:].rearrange("p t g -> p (t g)").unsqueeze(2).broadcast_to([P, NT * G, GE])))
            chain(ve.copy_predicated(masked[:].rearrange("p t (g e) -> p (t g) e", e=GE), emask[:], v))
            pick_top(rep[:], masked[:], 8)
            chain(ve.scalar_tensor_tensor(out=sel[:], in0=rep[:], scalar=-1e38, in1=score[:], op0=ALU.is_le, op1=ALU.mult))
            chain(ve.reduce_sum(red[:], sel[:], AX_X))
            chain(ve.tensor_scalar(red[:], red[:], 1e-20, None, ALU.add))
            chain(ve.reciprocal(rcp[:], red[:]))
            chain(ve.tensor_scalar(rcp[:], rcp[:], 2.5, None, ALU.mult))
            chain(ve.tensor_tensor(comb[:], sel[:], over_experts(rcp[:]), ALU.mult))
        ve.tensor_copy(stack[:, :, 0:E], comb[:]).then_inc(stacked, 1)
        ve.wait_ge(stacked, 1)
        ve.tensor_tensor(stack[:, :, 64:64 + E], comb[:], stack[:, :, 0:E].bitcast(F32), ALU.subtract).then_inc(stacked, 1)

    return Router(load=load, zero=zero, turn=turn, activate=activate, copy_turned=copy_turned, choose=choose, ready=ready)


def add_moe(nc, cfg, xT, h_hi, h_lo, logits, CT, gate, consts, dram):
    up, name = cfg.up, "m1" if cfg.rel else "m0"
    U = cfg.units + 2
    STEPS = U // 2
    SEL, DOWN = up, up + 1
    NSH = 2 * B
    with ExitStack() as ctx:
        sb = lambda n, s, d=F32: ctx.enter_context(nc.sbuf_tensor(f"{name}_{n}", s, d))
        sem = lambda n: nc.alloc_semaphore(f"{name}_{n}")
        ps = ctx.enter_context(nc.psum_tensor(f"{name}_ps", [P, 8, T], F32))
        w = [sb(f"w{q}", [P, up + 2, P]) for q in range(2)]
        w_hi = [sb(f"whi{q}", [P, up + 1, P], F32R) for q in range(2)]
        w_lo = [sb(f"wlo{q}", [P, up, P], F32R) for q in range(2)]
        acts = sb("acts", [P, B, T])
        scaled = sb("scaled", [P, B, T])
        hidden = sb("hidden", [P, B, T])
        w_loaded = [sem("wl0"), sem("wl1")]
        w_rounded, w_split = sem("wr"), sem("ws")
        up_ready, up2_ready, comb_ready, act_ready = sem("up"), sem("up2"), sem("cb"), sem("act")
        gated = sem("gt")
        scaled_ready, hidden_ready, down_done, added = sem("sc"), sem("hid"), sem("dn"), sem("add")
        A = lambda m: ps[:, 4 + m % 2, :]
        Bk = ps[:, 6, :]
        C = lambda m: ps[:, 6 + m % 2, :] if up == 1 else ps[:, 7, :]
        LAG = 2
        router = make_router(nc, ctx, cfg, logits, CT, lambda b: ps[:, 6 + b % 2, :], consts, dram)
        block = ctx.enter_context(nc.Block())

        def steps(eng, body, after_shared=None):
            body(0, False)
            if after_shared:
                after_shared(eng)
            with eng.Fori(1, STEPS - 1) as k:
                body(k, False)
            body(STEPS - 1, True)

        @block.sync
        def _(sp):
            def body(k, last):
                for q in range(2):
                    u = 2 * k + q
                    wait_past(sp, w_loaded[q], 16 * k)
                    wait_past(sp, down_done, B * u - B)
                    sp.dma_start(w[q][:], dram["units"][bass.ds(u, 1)].rearrange("o p (k m) -> p (o k) m", k=up + 2)).then_inc(w_loaded[q], 16)

            router.load(sp)
            steps(sp, body)

        @block.tensor
        def _(pe):
            def down(m, q, b, first):
                pe.wait_ge(hidden_ready, m + 1)
                pe.matmul(ps[:, b, :], w[q][:, DOWN, :], hidden[:, b, :], start=first, stop=False,
                          skip_group_check=True).then_inc(down_done, 1)

            def project(bank, q, a, tok):
                pe.matmul(bank, w_hi[q][:, a, :], h_hi[:, tok], start=True, stop=False)
                pe.matmul(bank, w_hi[q][:, a, :], h_lo[:, tok], start=False, stop=False)
                return pe.matmul(bank, w_lo[q][:, a, :], h_hi[:, tok], start=False, stop=True)

            def body(k, last):
                shared = isinstance(k, int) and k == 0
                for q in range(2):
                    u = 2 * k + q
                    for b in range(B):
                        m = B * u + b
                        tok = slice(b * T, (b + 1) * T)
                        if b == 0:
                            pe.wait_ge(w_split, u + 1)
                        wait_past(pe, act_ready, m - 1)
                        project(A(b), q, 0, tok).then_inc(up_ready, 1)
                        if up == 2:
                            wait_past(pe, gated, m)
                            project(Bk, q, 1, tok).then_inc(up2_ready, 1)
                        if not shared:
                            pe.wait_ge(hidden_ready, m - 1 if up == 1 else m)
                            pe.matmul(C(b), w_hi[q][:, SEL, :], CT[:, tok], start=True, stop=True).then_inc(comb_ready, 1)
                        if not (shared and m < LAG):
                            old = (b - LAG) % B
                            down(m - LAG, q if b >= LAG else 1 - q, old, first=shared and m - LAG < B)
                if last:
                    for b in range(B - LAG, B):
                        down(B * U - B + b, 1, b, False)

            def turn_weights(pe):
                if up == 2:
                    pe.wait_ge(gated, NSH)
                router.turn(pe)
                pe.wait_ge(router.ready, B)

            steps(pe, body, turn_weights)

        @block.scalar
        def _(act):
            def body(k, last):
                for q in range(2):
                    for b in range(B):
                        m = B * (2 * k + q) + b
                        act.wait_ge(up_ready, m + 1)
                        wait_past(act, hidden_ready, m + 1 - B)
                        act.activation(acts[:, b, :], A(b), ACT.Relu if up == 1 else ACT.Silu).then_inc(act_ready, 1)

            router.activate(act)
            steps(act, body, router.copy_turned)

        def split(ve, u, k, q):
            ve.wait_ge(w_loaded[q], 16 * (k + 1))
            wait_past(ve, hidden_ready, B * (u - 1))
            ve.tensor_copy(w_hi[q][:], w[q][:, 0:up + 1, :]).then_inc(w_rounded, 1)
            ve.wait_ge(w_rounded, u + 1)
            ve.tensor_tensor(w_lo[q][:], w[q][:, 0:up, :], w_hi[q][:, 0:up, :].bitcast(F32), ALU.subtract).then_inc(w_split, 1)

        @block.vector
        def _(ve):
            split(ve, 0, 0, 0)
            split(ve, 1, 0, 1)
            router.choose(ve)

            def body(k, last):
                shared = isinstance(k, int) and k == 0
                for q in range(2):
                    u = 2 * k + q
                    for b in range(B):
                        m = B * u + b
                        if b == 3 and not (last and q == 1) and not (shared and q == 0):
                            split(ve, u + 1, k + q, 1 - q)
                        if up == 2:
                            ve.wait_ge(act_ready, m + 1)
                            ve.wait_ge(up2_ready, m + 1)
                            if shared:
                                wait_past(ve, down_done, m + 1 - B)
                                ve.tensor_tensor(hidden[:, b, :], Bk, acts[:, b, :], ALU.mult).then_inc(gated, 1)
                                ve.wait_ge(gated, m + 1)
                                ve.sem_inc(hidden_ready, 1)
                                continue
                            ve.tensor_tensor(scaled[:, b, :], Bk, acts[:, b, :], ALU.mult).then_inc(gated, 1)
                            ve.wait_ge(comb_ready, m + 1 - NSH)
                            ve.wait_ge(gated, m + 1)
                            ve.wait_ge(down_done, m + 1 - B)
                            ve.tensor_tensor(hidden[:, b, :], C(b), scaled[:, b, :], ALU.mult).then_inc(hidden_ready, 1)
                        elif not shared:
                            ve.wait_ge(act_ready, m + 1)
                            ve.wait_ge(comb_ready, m + 1 - NSH)
                            ve.wait_ge(hidden_ready, m + 1 - B)
                            ve.tensor_tensor(scaled[:, b, :], C(b), acts[:, b, :], ALU.mult).then_inc(scaled_ready, 1)

            steps(ve, body)
            for b in range(B):
                ve.wait_ge(down_done, B * (U - 1) + b + 1)
                s = slice(b * T, (b + 1) * T)
                ve.scalar_tensor_tensor(out=xT[:, s], in0=ps[:, b, :], scalar=gate[:, b:b + 1], in1=xT[:, s],
                                        op0=ALU.mult, op1=ALU.add).then_inc(added, 1)

        @block.gpsimd
        def _(pool):
            router.zero(pool)
            if up == 2:
                return

            def body(k, last):
                shared = isinstance(k, int) and k == 0
                for q in range(2):
                    for b in range(B):
                        m = B * (2 * k + q) + b
                        wait_past(pool, down_done, m + 1 - B)
                        pool.wait_ge(act_ready, m + 1)
                        other = acts if shared else scaled
                        if not shared:
                            pool.wait_ge(scaled_ready, m + 1 - NSH)
                        pool.tensor_tensor(hidden[:, b, :], acts[:, b, :], other[:, b, :], ALU.mult).then_inc(hidden_ready, 1)

            steps(pool, body)


N_CONST = 3 * P + HG + 2 * DIAG + 4 * T + 2


def build_program(nc, a, out, upto=99):
    with ExitStack() as ctx:
        sb = lambda n, s, d=F32: ctx.enter_context(nc.sbuf_tensor(n, s, d))
        xT, hT = sb("xT", [P, NTOK]), sb("hT", [P, NTOK])
        const = sb("const", [P, N_CONST])
        bf = sb("const_bf", [P, 2, P], BF16)
        mods = [sb(f"mod{k}", [P, 6, B]) for k in range(2)]
        mean_w, eps_col = sb("mean_w", [P, 1]), sb("eps", [P, 1])
        gate_w = [sb("gate0", [P, 8]), sb("gate1", [P, 64])]
        wv, gb, bv = [sb(f"wv{k}", [P, D]) for k in range(2)], sb("ln_gb", [P, 2]), sb("bv", [P, D])
        load_done, wp_loaded, out_done = (nc.alloc_semaphore(n) for n in ("load_done", "wp_loaded", "out_done"))
        vall = sb("vall", [P, B * NB, H, QW])
        qz = [sb(f"qz{p}", [P, HG, T], F32R) for p in range(2)]
        diag = sb("diag", [P, NB, T])
        wp_all = sb("wp_all", [P, NG, HG * 2 * P], F32R)

        consts, at = {}, 0
        for key, n in (("ident", P), ("causal_f", P), ("pick", HG), ("lower", DIAG), ("upper_f", DIAG), ("pe", 2 * T), ("cos", T), ("sin", T),
                       ("neg_lo_q", 1), ("neg_lo_k", 1), ("centre", P)):
            consts[key] = const[:, at:at + n]
            at += n
        upper = sb("upper", [P, DIAG], U32)
        consts["upper"] = upper[:]
        consts["ident_bf"], consts["causal"] = bf[:, 0, :], bf[:, 1, :]

        def start_sync(sp):
            for dst, src in ((xT[:], a["xT"]), (const[:, 0:at], a["const"]), (wv[0][:], a["wv0"]), (wv[1][:], a["wv1"]),
                             (gb[:], a["ln_gb"]), (bv[:], a["bv"]), (gate_w[0][:], a["gate0"]), (gate_w[1][:], a["gate1"])):
                sp.dma_start(dst, src).then_inc(load_done, 16)
            sp.wait_ge(load_done, 128)
            sp.dma_start(wp_all[:].bitcast(F32), a["wp1"].rearrange("g p m -> p g m")).then_inc(wp_loaded, 16)

        def start_vector(ve):
            ve.memset(mean_w[:], 1.0 / D)
            ve.memset(eps_col[:], LN_EPS)
            ve.wait_ge(load_done, 128)
            ve.tensor_copy(bf[:, 0, :], consts["ident"])
            ve.tensor_copy(bf[:, 1, :], consts["causal_f"])
            ve.tensor_copy(upper[:], consts["upper_f"])

        def start_gpsimd(pool):
            pool.memset(vall[:, :, :, 0:DH + 1], 1.0)
            pool.memset(vall[:, :, :, DH + 1:QW], 0.0)
            for q in qz:
                pool.memset(q[:].bitcast(F32), 0.0)
            pool.memset(diag[:], 0.0)

        counts = {}
        add_modulation(nc, [(a["c0"], a["wmod0"], mods[0]), (a["c1"], a["wmod1"], mods[1])], start_sync, start_vector, start_gpsimd)

        for k, cfg in enumerate((Cfg(False), Cfg(True))):
            mod = mods[k]
            shift = lambda j, mod=mod: (lambda b: mod[:, j, b:b + 1])
            if upto < 4 * k + 1:
                break
            ln = (consts["centre"], mean_w[:], consts["ident"], eps_col, counts)
            v_out = lambda b: vall[:, b * NB:(b + 1) * NB, :, 0:DH]
            by_head = lambda ap: ap.rearrange("p t (h d) -> p t h d", d=DH)
            if cfg.rel:
                add_layernorm(nc, f"ln{k}m", xT, hT, shift(1), shift(0), *ln)
                add_layernorm(nc, f"ln{k}a", hT, hT, lambda b: gb[:, 0:1], lambda b: gb[:, 1:2], *ln, wt=wv[k][:], wt_out=v_out,
                              wt_view=by_head, wt_bias=by_head(bv[:].unsqueeze(1).broadcast_to([P, NB, D])))
            else:
                add_layernorm(nc, f"ln{k}a", xT, hT, shift(1), shift(0), *ln, wt=wv[k][:], wt_out=v_out, wt_view=by_head)
            if upto < 4 * k + 2:
                break
            add_attention(nc, cfg, xT, hT, vall, qz, diag, wp_all, wp_loaded, mod[:, 2, :], consts,
                          {n: a.get(f"{n}{k}") for n in ("wqk", "wo", "cols")})
            if upto < 4 * k + 3:
                break
            with nc.sbuf_tensor(f"hhi{k}", [P, NTOK], F32R) as h_hi, nc.sbuf_tensor(f"hlo{k}", [P, NTOK], F32R) as h_lo, \
                    nc.sbuf_tensor(f"CT{k}", [P, NTOK], F32R) as CT:
                with nc.sbuf_tensor(f"logits{k}", [P, B * NB, cfg.E], F32) as logits:
                    add_layernorm(nc, f"ln{k}f", xT, hT, shift(4), shift(3), *ln, dst_hi=h_hi, dst_lo=h_lo, wt=gate_w[k][:],
                                  wt_out=lambda b, logits=logits: logits[:, b * NB:(b + 1) * NB, :])
                    add_moe(nc, cfg, xT, h_hi, h_lo, logits, CT, mod[:, 5, :], consts, {"units": a[f"units{k}"], "bias": a[f"bias{k}"]})

        with nc.Block() as block:
            @block.sync
            def _(sp):
                res = hT if upto in (1, 5) else xT
                sp.dma_start(out, res[:]).then_inc(out_done, 16)
                sp.wait_ge(out_done, 16)


def constants():
    ident = np.eye(P)
    i, j = np.arange(P)[:, None], np.arange(P)[None, :]
    causal = np.where(j > i, NEG, 0.0)
    pick = (i == j[:, :HG] * QW + DH).astype(float)
    jd = np.arange(DIAG)[None, :]
    tri = np.concatenate([(jd <= i), (jd >= i + 2)], 1).astype(float)
    div = np.exp(np.arange(0, D, 2, dtype=np.float32) * np.float32(-np.log(10000.0) / D)).astype(np.float64)
    w = np.repeat(div, 2)[:, None]
    odd = (np.arange(D) % 2)[:, None]
    x = np.concatenate([np.arange(T), T + np.arange(T)])[None, :]
    pe = np.where(odd == 1, np.cos(w * x), np.sin(w * x))
    r = np.arange(1, T + 1)[None, :]
    cos, sin = np.cos(w * r), np.sin(w * r) * np.where(odd == 1, -1.0, 1.0)
    row = np.arange(P)[:, None] % QW // DH
    return np.concatenate([ident, causal, pick, tri, pe, cos, sin, -1.0 * (row == 1), -1.0 * (row == 2), ident - 1.0 / D], 1).astype(np.float32)


def stacked_columns(w):
    w = w.reshape(w.shape[0], NG, HG, 1, DH)
    z = np.zeros_like(w)
    return np.concatenate([w, w, w, z], 3).reshape(w.shape[0], NG, P).transpose(1, 0, 2)


def selectors(units, up):
    s = np.zeros((units + 2, P, P), np.float32)
    for u in range(units):
        for m in range(P):
            e = u // 2 if up == 2 else 2 * u + m // 64
            s[u + 2, e, m] = s[u + 2, 64 + e, m] = 1.0
    return s


def pack_units(ups, sel, down):
    return np.ascontiguousarray(np.concatenate([*ups, sel, down], 2))


def lay_out(d):
    f = {k: np.asarray(v) for k, v in d.items()}
    a = {"xT": f["L0_attn_x"].reshape(NTOK, D).T, "const": constants(), "ln_gb": np.stack([f["L1_attn_ln_g"], f["L1_attn_ln_b"]], 1)}
    for k in range(2):
        p = f"L{k}_attn_"
        a[f"c{k}"], a[f"wmod{k}"] = f[f"L{k}_c"].T, f[f"L{k}_wmod"]
        a[f"wv{k}"] = f[p + "Wv"]
        a[f"wqk{k}"] = np.concatenate([stacked_columns(f[p + "Wq"]), stacked_columns(f[p + "Wk"])], 2)
        wo = f[p + "Wo"].reshape(NG, HG, DH, D)
        a[f"wo{k}"] = np.concatenate([wo, np.zeros((NG, HG, QW - DH, D), np.float32)], 2).reshape(NG, P, D)
    p = "L1_attn_"
    wp = f[p + "Wp"]
    swapped = wp.reshape(D // 2, 2, D)[:, ::-1].reshape(D, D)
    both = np.stack([stacked_columns(wp), stacked_columns(swapped)])
    both = both.reshape(2, NG, D, HG, QW)
    z = np.zeros((NG, HG, QW, HG, 2, D), np.float32)
    for h in range(HG):
        z[:, h, :, h] = both[:, :, :, h].transpose(1, 3, 0, 2)
    a["wp1"] = z.reshape(NG, P, HG * 2 * D)
    col = lambda v: stacked_columns(v.reshape(1, D))[:, 0, :].T
    a["cols1"] = np.stack([col(f[p + "bq"]), col(f[p + "u_bias"]), col(f[p + "v_bias"]), col(f[p + "bk"]),
                           np.repeat(f[p + "bo"][:, None], NG, 1)], 1)
    a["bv"] = np.broadcast_to(f[p + "bv"], (P, D))
    a["gate0"], a["gate1"] = f["L0_ffn_gate_w"].T, f["L1_ffn_router_w"].T
    a["bias0"] = np.broadcast_to(f["L0_ffn_gate_bias"], (P, 8))
    a["bias1"] = np.broadcast_to(f["L1_ffn_correction_bias"], (P, 64))
    halves = lambda shared, w: np.concatenate([shared[None], w]).reshape(-1, P, D)
    w1, w3 = (halves(f[f"L0_ffn_s{n}"], f[f"L0_ffn_{n}"]).transpose(0, 2, 1) for n in ("w1", "w3"))
    w2 = np.concatenate([f["L0_ffn_sw2"][None], f["L0_ffn_w2"]]).transpose(0, 2, 1).reshape(-1, P, D)
    a["units0"] = pack_units([w1, w3], selectors(16, 2), w2)
    up = f["L1_ffn_up_w"].reshape(32, 2, D, 64).transpose(0, 2, 1, 3).reshape(32, D, P)
    sup = f["L1_ffn_shared_up_w"].reshape(D, 2, P).transpose(1, 0, 2)
    down = f["L1_ffn_down_w"].reshape(32, P, D)
    sdown = f["L1_ffn_shared_down_w"].reshape(2, P, D)
    a["units1"] = pack_units([np.concatenate([sup, up])], selectors(32, 1), np.concatenate([sdown, down]))
    return {k: np.ascontiguousarray(v) for k, v in a.items()}


def kernel(**inputs):
    import concourse.bacc as bacc
    from concourse.bass_utils import run_bass_kernel_spmd

    nc = bacc.Bacc("TRN2", target_bir_lowering=False, num_devices=1)
    arrays = lay_out(inputs)
    aps = {k: nc.dram_tensor(f"in_{k}", v.shape, mybir.dt.from_np(v.dtype), kind="ExternalInput").ap() for k, v in arrays.items()}
    out = nc.dram_tensor("out_xT", (P, NTOK), F32, kind="ExternalOutput").ap()
    build_program(nc, aps, out)
    r = run_bass_kernel_spmd(nc, [{f"in_{k}": v for k, v in arrays.items()}], core_ids=[0])
    return np.ascontiguousarray(r.results[0]["out_xT"].T).reshape(B, T, D)
```
